# Optimizing a Trainium2 kernel written in Bass

```python
import numpy as np
import jax
import jax.numpy as jnp

def _softmax(x, axis=-1):
    return jax.nn.softmax(x, axis=axis)

def _gelu(x):
    return jax.nn.gelu(x, approximate=True)

def _silu(x):
    return jax.nn.silu(x)

def _sigmoid(x):
    return jax.nn.sigmoid(x)

def _layernorm(x, axis=-1, eps=1e-05):
    m = jnp.mean(x, axis=axis, keepdims=True)
    v = jnp.var(x, axis=axis, keepdims=True)
    return (x - m) / jnp.sqrt(v + eps)

def _scatter_add(tgt, idx, src, axis=0):
    return tgt.at[idx].add(src)

def _segment_sum(src, seg, n):
    return jax.ops.segment_sum(src, seg, n)
kernel_name = 'mk_seq_postln_d1_jaxref_r8_20e676'

def setup_inputs(seed: int=0):
    np.random.seed(seed)
    _w = jnp.asarray

    def _L0_attn_setup():
        import jax, jax.numpy as jnp
        import numpy as np
        N_HEAD = 32
        ROPE_BASE = 10000.0

        def _rope_cos_sin(T, n_elem, dtype):
            theta = 1.0 / ROPE_BASE ** (jnp.arange(0, n_elem, 2, dtype=dtype) / n_elem)
            seq_idx = jnp.arange(T, dtype=dtype)
            idx_theta = jnp.outer(seq_idx, theta)
            idx_theta2 = jnp.concatenate([idx_theta, idx_theta], axis=-1)
            return (jnp.cos(idx_theta2), jnp.sin(idx_theta2))

        def _apply_rope(x, cos, sin):
            d2 = x.shape[-1] // 2
            rot = jnp.concatenate([-x[..., d2:], x[..., :d2]], axis=-1)
            return x * cos + rot * sin
        key = jax.random.key(seed)
        k1, k2, k3, k4 = jax.random.split(key, 4)
        B, T, C = (1, 256, 512)
        s_in = 1.0 / np.sqrt(C)
        return {'x': jax.random.normal(k1, (B, T, C), jnp.float32), 'w_attn': jax.random.normal(k2, (3 * C, C), jnp.float32) * s_in, 'w_proj': jax.random.normal(k3, (C, C), jnp.float32) * s_in, 'adapter_wte': jax.random.normal(k4, (10, C), jnp.float32), 'gating': jnp.ones((1,), jnp.float32)}
    _L0_attn_in = _L0_attn_setup()

    def _L0_ffn_setup():
        import jax, jax.numpy as jnp
        import numpy as np
        TOP_K = 2
        SCALING = 32.0 / 64.0
        key = jax.random.key(seed)
        ks = jax.random.split(key, 6)
        Bsz, S, Din, Dout, R, E = (4, 256, 512, 512, 64, 16)
        x = jax.random.normal(ks[0], (Bsz, S, Din), dtype=jnp.float32)
        base_w = jax.random.normal(ks[1], (Dout, Din), dtype=jnp.float32) * 0.02
        base_b = jax.random.normal(ks[2], (Dout,), dtype=jnp.float32) * 0.02
        A = jax.random.normal(ks[3], (R, Din), dtype=jnp.float32) * (1.0 / np.sqrt(Din))
        B = jax.random.normal(ks[4], (E, Dout, R), dtype=jnp.float32) * 0.02
        router_w = jax.random.normal(ks[5], (E, Din), dtype=jnp.float32) * 0.02
        return {'x': x, 'base_w': base_w, 'base_b': base_b, 'A': A, 'B': B, 'router_w': router_w}
    _L0_ffn_in = _L0_ffn_setup()
    _d = {'L0_attn_x': _L0_attn_in['x'], 'L0_attn_w_attn': _L0_attn_in['w_attn'], 'L0_attn_w_proj': _L0_attn_in['w_proj'], 'L0_attn_adapter_wte': _L0_attn_in['adapter_wte'], 'L0_attn_gating': _L0_attn_in['gating'], 'L0_ffn_base_w': _L0_ffn_in['base_w'], 'L0_ffn_base_b': _L0_ffn_in['base_b'], 'L0_ffn_A': _L0_ffn_in['A'], 'L0_ffn_B': _L0_ffn_in['B'], 'L0_ffn_router_w': _L0_ffn_in['router_w']}
    _x0 = _d['L0_attn_x']
    _d['L0_attn_x'] = jax.random.normal(jax.random.fold_in(jax.random.key(seed), 1), (2, 1024, 512), dtype=_x0.dtype)
    del _x0
    return _d

def reference(L0_attn_x, L0_attn_w_attn, L0_attn_w_proj, L0_attn_adapter_wte, L0_attn_gating, L0_ffn_base_w, L0_ffn_base_b, L0_ffn_A, L0_ffn_B, L0_ffn_router_w):

    def _L0_attn_ref(x, w_attn, w_proj, adapter_wte, gating):
        import jax, jax.numpy as jnp
        import numpy as np
        N_HEAD = 32
        ROPE_BASE = 10000.0

        def _rope_cos_sin(T, n_elem, dtype):
            theta = 1.0 / ROPE_BASE ** (jnp.arange(0, n_elem, 2, dtype=dtype) / n_elem)
            seq_idx = jnp.arange(T, dtype=dtype)
            idx_theta = jnp.outer(seq_idx, theta)
            idx_theta2 = jnp.concatenate([idx_theta, idx_theta], axis=-1)
            return (jnp.cos(idx_theta2), jnp.sin(idx_theta2))

        def _apply_rope(x, cos, sin):
            d2 = x.shape[-1] // 2
            rot = jnp.concatenate([-x[..., d2:], x[..., :d2]], axis=-1)
            return x * cos + rot * sin
        B, T, C = x.shape
        H = N_HEAD
        hd = C // H
        qkv = jnp.einsum('btc,oc->bto', x, w_attn)
        q, k, v = jnp.split(qkv, 3, axis=-1)
        q = q.reshape(B, T, H, hd).transpose(0, 2, 1, 3)
        k = k.reshape(B, T, H, hd).transpose(0, 2, 1, 3)
        v = v.reshape(B, T, H, hd).transpose(0, 2, 1, 3)
        cos, sin = _rope_cos_sin(T, hd, x.dtype)
        q = _apply_rope(q, cos, sin)
        k = _apply_rope(k, cos, sin)
        scores = jnp.einsum('bhqd,bhkd->bhqk', q, k) / jnp.sqrt(jnp.asarray(hd, x.dtype))
        causal = jnp.tril(jnp.ones((T, T), bool))
        scores = jnp.where(causal, scores, jnp.asarray(-jnp.inf, x.dtype))
        attn = jax.nn.softmax(scores, axis=-1)
        y = jnp.einsum('bhqk,bhkd->bhqd', attn, v)
        aT = adapter_wte.shape[0]
        prefix = adapter_wte[None]
        aqkv = jnp.einsum('btc,oc->bto', prefix, w_attn)
        _, ak, av = jnp.split(aqkv, 3, axis=-1)
        ak = ak.reshape(1, aT, H, hd).transpose(0, 2, 1, 3)
        av = av.reshape(1, aT, H, hd).transpose(0, 2, 1, 3)
        ascores = jnp.einsum('bhqd,xhkd->bhqk', q, ak) / jnp.sqrt(jnp.asarray(C, x.dtype))
        ascores = gating[0] * jax.nn.softmax(ascores.astype(jnp.float32), axis=-1).astype(q.dtype)
        y = y + jnp.einsum('bhqk,xhkd->bhqd', ascores, av)
        y = y.transpose(0, 2, 1, 3).reshape(B, T, C)
        return jnp.einsum('btc,oc->bto', y, w_proj)

    def _L0_ffn_ref(x, base_w, base_b, A, B, router_w):
        import jax, jax.numpy as jnp
        import numpy as np
        TOP_K = 2
        SCALING = 32.0 / 64.0
        base_out = jnp.einsum('bsi,oi->bso', x, base_w) + base_b
        res_hidden = jnp.einsum('bsi,ri->bsr', x, A)
        logits = jnp.einsum('bsi,ei->bse', x, router_w)
        probs = jax.nn.softmax(logits, axis=-1)
        topw, topi = jax.lax.top_k(probs, TOP_K)
        topw = topw / (jnp.sum(topw, axis=-1, keepdims=True) + 1e-06)
        num_experts = B.shape[0]
        combine = jnp.sum(jax.nn.one_hot(topi, num_experts, dtype=x.dtype) * topw[..., None], axis=-2)
        delta = jnp.einsum('bse,bsr,eor->bso', combine, res_hidden, B)
        return base_out + delta * SCALING
    x = L0_attn_x
    x = _layernorm(x + _L0_attn_ref(x, L0_attn_w_attn, L0_attn_w_proj, L0_attn_adapter_wte, L0_attn_gating), axis=-1)
    x = _layernorm(x + _L0_ffn_ref(x, L0_ffn_base_w, L0_ffn_base_b, L0_ffn_A, L0_ffn_B, L0_ffn_router_w), axis=-1)
    return x

_drawn_inputs = setup_inputs


def setup_inputs(seed=0):
    import zlib

    import numpy as np

    out = dict(_drawn_inputs(seed))
    spreads = {}
    factors = {'L0_ffn_base_b': 3.179}
    for name, (base, spread) in spreads.items():
        noise = np.random.default_rng([zlib.crc32(name.encode()), seed]).standard_normal(out[name].shape)
        drawn = base * np.exp(spread * noise) if base else spread * noise
        out[name] = jnp.asarray(drawn.astype(out[name].dtype))
    for name, factor in factors.items():
        out[name] = (out[name] * factor).astype(out[name].dtype)
    return out
```

```python
from contextlib import ExitStack

import concourse.bass as bass
from concourse import mybir

F32 = mybir.dt.float32
F32R = mybir.dt.float32r
I32 = mybir.dt.int32
BF16 = mybir.dt.bfloat16
ALU = mybir.AluOpType
ACT = mybir.ActivationFunctionType
AX = mybir.AxisListType

NB, T, C, H = 2, 1024, 512, 32
HD = C // H
J = 10
E, R = 16, 64
P = 128
CC = C // P
TT = 512
NTT = T // TT
HG = 4
GB = H // HG
G = NB * GB
QT = T // P
PARTS = 3
TERMS = [(0, 0), (0, 1), (0, 2), (1, 0), (1, 1), (2, 0)]
KR = len(TERMS) * HD
KX = KR + 2
NEG = -3.0e38
VW = 32
EPS = 1e-5
NEWTON = 3
NORM_STEPS = 4 + 3 * NEWTON


HEAD_START = {"yadd": ("gp", 3), "uf": ("pe", 4), "tm": ("ve", 8), "ro": ("ve", 2), "rem": ("gp", 2), "p3": ("gp", 2), "vr": ("act", 2),
              "asub": ("ve", 2), "xh": ("act", 2), "xl": ("ve", 2), "pst0": ("sp", 16), "pst1": ("sp", 16)}


MAX_BANKS = [
    [(0, 0, 1), (2, 0, 3)],
    [(1, 0, 2), (5, 4, 2)],
    [(3, 0, 4)],
    [(4, 0, 4)],
    [(4, 4, 1), (6, 4, 3)],
    [(5, 0, 4)],
    [(6, 0, 4)],
    [(7, 0, 4)],
    [(7, 4, 4)],
]
NMB = len(MAX_BANKS)
NMX = HG * NMB
LEAD = NMB
NORM = [(0, 3), (3, 3), (6, 2)]
ROWS_LAG = 3
LAG = 2
NORM_COLUMNS = 800
BANK_EVERY = (HG * P * QT * (QT + 1) - len(NORM) * NORM_COLUMNS) // NMX
NTC = NB * QT
CW = [("w_projT", 0), ("base_wT", 0), ("arT", 0), ("B_T", 0), ("B_T", CC)]


def runs(pick):
    out, r = [], 0
    while r < len(TERMS):
        n = 1
        while r + n < len(TERMS) and TERMS[r + n][pick] == TERMS[r + n - 1][pick] + 1:
            n += 1
        out.append((r, n, TERMS[r][pick]))
        r += n
    return out


GROUP_LOADS = len(runs(0)) + len(runs(1))


class Group:

    def __init__(self, g, m, v):
        self.g, self.m, self.v, self.fixed = g, m, v, isinstance(g, int)

    def plus(self, n):
        return Group(self.g + n, (self.m + n) % 3, self.v + (self.m + n) // 3)

    def has(self, n):
        return not self.fixed or 0 <= self.g + n < G


def value_pieces(kb):
    spans = [(max(c0, kb * P), c0 + 512) for c0 in (0, 512) if kb * P < c0 + 512]
    return [(q0, q1, h, (q0, h) == (spans[-1][0], 2)) for q0, q1 in spans for h in (0, 2)]


def items(gr):
    todo = ([(1, w) for w in range(LEAD, NMX)] if gr.has(1) else []) + ([(2, w) for w in range(LEAD)] if gr.has(2) else [])
    out, off, rows_in = [], 0, None

    def bank_items(n):
        nonlocal off, rows_in
        for _ in range(n):
            if rows_in == 0 or (rows_in is not None and not todo):
                out.append(("rows", 1, off))
                off += 1
                rows_in = None
            if not todo:
                return
            n_, w = todo.pop(0)
            out.append(("max", n_, w, off))
            off += 1
            if rows_in is not None:
                rows_in -= 1
            if (n_, w) == (1, NMX - 1):
                out.append(("calc", 1, off))
                rows_in = ROWS_LAG

    due = 0
    for kb in range(QT):
        if kb >= LAG:
            values = [(0, kb - LAG) + p for p in value_pieces(kb - LAG)]
        else:
            values = [(-1, QT - LAG + kb) + p for p in value_pieces(QT - LAG + kb)] if gr.has(-1) else []
        for h in range(HG):
            work = [(("score", kb, h), T - kb * P)]
            n = len(values)
            for v in values[n * h // HG:n * (h + 1) // HG]:
                work.append((("pv",) + v, 2 * (v[3] - v[2])))
            for it, columns in work:
                out.append(it)
                due += columns
                while due >= BANK_EVERY:
                    bank_items(1)
                    due -= BANK_EVERY
            if kb == 3 and h < len(NORM) and gr.has(-1):
                out.append(("norm", h, off))
                off += 1
                due -= NORM_COLUMNS
    bank_items(NMX)
    if rows_in is not None:
        bank_items(1)
    return out, off


PRO = NMX + 1 + (LEAD if G > 1 else 0)
USE0 = [PRO]
for _g in range(G):
    USE0.append(USE0[-1] + items(Group(_g, _g % 3, _g // 3))[1])
STEADY = USE0[2] - USE0[1]
assert STEADY % 2 == 0 and all(USE0[n + 1] - USE0[n] == STEADY for n in range(1, G - 2))
PSM_TOTAL = USE0[G] + len(NORM)


def use_of(gr, off):
    if gr.fixed:
        return USE0[gr.g] + off, (USE0[gr.g] + off) % 2
    return gr.g * STEADY + (USE0[1] - STEADY + off), (USE0[1] + off) % 2


def norm_end(gr):
    offs = [x[2] for x in items(gr)[0] if x[0] == "norm"]
    return use_of(gr, offs[-1] + 1)[0]


def drive(eng, group):
    group(Group(0, 0, 0))
    with eng.Fori(0, 4) as i:
        for k in range(1, 4):
            group(Group(3 * i + k, k % 3, i + k // 3))
    for g in range(13, G):
        group(Group(g, g % 3, g // 3))


def drive_tiles(eng, step):
    for j in range(4):
        step(j, j % 2)
    with eng.Fori(0, NTC // 2 - 3) as i:
        for k in range(2):
            step(2 * i + (4 + k), k)
    for j in range(NTC - 2, NTC + 2):
        step(j, j % 2)


def build(nc, d):
    with ExitStack() as ctx:
        def sem(name):
            return ctx.enter_context(nc.semaphore(name))

        def psum(name, cols, dt=F32):
            return ctx.enter_context(nc.psum_tensor(name, [P, cols], dt))

        def sb(stack, name, shape, dt=F32):
            return stack.enter_context(nc.sbuf_tensor(name, shape, dt))

        q_parts = nc.dram_tensor("q_parts", (NB * H, PARTS, HD, T), BF16, kind="Internal").ap()
        k_parts = nc.dram_tensor("k_parts", (NB * H, PARTS, HD, T), BF16, kind="Internal").ap()

        ident = sb(ctx, "ident", [P, P])
        identb = sb(ctx, "identb", [P, P], BF16)
        cmask = sb(ctx, "cmask", [P, P])
        v_all = sb(ctx, "v_all", [P, G, QT, HG * HD])
        y_all = sb(ctx, "y_all", [P, G, QT, HG * HD])

        with ExitStack() as a:
            cs = sb(a, "cs", [P, 2, T])
            wh = sb(a, "wh", [P, CC, 3 * C], F32R)
            wl = sb(a, "wl", [P, CC, 3 * C], F32R)
            xs = sb(a, "xs", [P, 2, TT])
            xh = [sb(a, f"xh{i}", [P, CC, TT], F32R) for i in range(2)]
            xl = [sb(a, f"xl{i}", [P, CC, TT], F32R) for i in range(2)]
            rope = [sb(a, f"rope{i}", [P, 2, TT]) for i in range(2)]
            rtmp = [sb(a, f"rtmp{i}", [P, TT]) for i in range(2)]
            rem = sb(a, "rem", [P, 2, TT])
            part = [sb(a, f"part{i}", [P, PARTS, 2, TT], BF16) for i in range(2)]
            pat = [sb(a, f"pat{i}", [80, 4, P]) for i in range(2)]
            gate = sb(a, "gate", [P, 1])
            akm = sb(a, "akm", [P, 16])
            avm = sb(a, "avm", [80, 8])
            akbd = sb(a, "akbd", [P, 2, 2, 16, J])
            avbd = sb(a, "avbd", [80, 4, P])
            asum = sb(a, "asum", [P, 4, H])
            with ExitStack() as a0:
                at_raw = sb(a0, "at_raw", [P, CC, J])
                ath = sb(a0, "ath", [P, CC, 80], F32R)
                atl = sb(a0, "atl", [P, CC, 80], F32R)
            with ExitStack() as a1:
                asb = [sb(a1, f"asb{i}", [P, H, J]) for i in range(2)]
                pa = [sb(a1, f"pa{i}", [P, H, J]) for i in range(4)]
        with ExitStack() as b:
            qs = [sb(b, f"qs{i}", [P, HG, T], BF16) for i in range(3)]
            ks = [sb(b, f"ks{i}", [P, HG, T], BF16) for i in range(3)]
            pt = [sb(b, f"pt{i}", [P, HG, T]) for i in range(3)]
            vb = [sb(b, f"vb{i}", [P, QT, HG, VW]) for i in range(3)]
            yts = sb(b, "yts", [P, T])
            mx = [sb(b, f"mx{i}", [P, 3, HG, QT]) for i in range(3)]
            mall = sb(b, "mall", [P, HG * QT])
            mneg = sb(b, "mneg", [P, 2, HG * QT], BF16)
            mrow = [sb(b, f"mrow{i}", [2 * HG * QT, P], BF16) for i in range(3)]
            rden = sb(b, "rden", [P, QT, HG])
            ynew = sb(b, "ynew", [P, QT, HG, HD])
        with ExitStack() as c:
            wph = sb(c, "wph", [P, CC, C], F32R)
            wpl = sb(c, "wpl", [P, CC, C], F32R)
            wfh = sb(c, "wfh", [P, CC, C], F32R)
            wfl = sb(c, "wfl", [P, CC, C], F32R)
            wbh = sb(c, "wbh", [P, 8, C], F32R)
            wbl = sb(c, "wbl", [P, 8, C], F32R)
            arh = sb(c, "arh", [P, CC, R + E], F32R)
            arl = sb(c, "arl", [P, CC, R + E], F32R)
            xin = [sb(c, f"xin{i}", [P, C]) for i in range(2)]
            ytile = [sb(c, f"ytile{i}", [P, C]) for i in range(2)]
            yth = [sb(c, f"yth{i}", [P, CC, P], F32R) for i in range(2)]
            ytl = [sb(c, f"ytl{i}", [P, CC, P], F32R) for i in range(2)]
            xth = [sb(c, f"xth{i}", [P, CC, P], F32R) for i in range(2)]
            xtl = [sb(c, f"xtl{i}", [P, CC, P], F32R) for i in range(2)]
            x1 = [sb(c, f"x1_{i}", [P, C]) for i in range(2)]
            xb = [sb(c, f"xb{i}", [P, C]) for i in range(2)]
            bias = sb(c, "bias", [P, C])
            gbuf = [sb(c, f"g{i}", [P, E, R]) for i in range(2)]
            gth = sb(c, "gth", [P, 8, P], F32R)
            gtl = sb(c, "gtl", [P, 8, P], F32R)
            outb = [sb(c, f"outb{i}", [P, C]) for i in range(2)]
            hr = [sb(c, f"hr{i}", [P, R]) for i in range(2)]
            ex = [sb(c, f"ex{i}", [P, E]) for i in range(2)]
            rev = sb(c, "rev", [P, E])
            sm = sb(c, "sm", [P, 72])
            rt = sb(c, "rt", [P, 8, E])
            comb = [sb(c, f"comb{i}", [P, E]) for i in range(2)]

        bank = [psum(f"bank{i}", 2 * 512) for i in range(4)]

        def half(i, dt=None):
            return bank[i // 2][:, 512 * (i % 2):512 * (i % 2) + 512]

        block = ctx.enter_context(nc.Block())
        s = {}

        def at(eng, name, value, apart=False):
            if isinstance(value, int) and value <= 0:
                return
            value = value + HEAD_START.get(name, (None, 0))[1]
            eng.wait_ge(S(name), value)
            if apart and not isinstance(value, int):
                eng.sem_inc(S("carrier"), 1)

        def give_head_start(eng, who):
            for name, (by, n) in HEAD_START.items():
                if by == who:
                    eng.nop().then_inc(S(name), n)

        def S(name):
            if name not in s:
                s[name] = sem(name)
            return s[name]

        def three(pe, out, lh, ll, rh, rl, first, last):
            pe.matmul(out, lh, rh, start=first, stop=False)
            pe.matmul(out, ll, rh, start=False, stop=False)
            return pe.matmul(out, lh, rl, start=False, stop=last)

        NU = 4
        NV = 12
        TILES = NB * NTT
        xT_d = d["xT"].rearrange("(c p) t -> p c t", p=P)
        wT_d = d["w_attnT"].rearrange("(c p) n -> p c n", p=P)
        y_flat = y_all[:].rearrange("p g q n -> p (g q n)")
        v_flat = v_all[:].rearrange("p g q n -> p (g q n)")
        wst = [v_flat[:, i * CC * C:(i + 1) * CC * C].rearrange("p (c n) -> p c n", c=CC) for i in range(2)]

        def cw_dst(n):
            return [(wph[:], wpl[:], C), (wfh[:], wfl[:], C), (arh[:], arl[:], R + E),
                    (wbh[:, 0:CC], wbl[:, 0:CC], C), (wbh[:, CC:], wbl[:, CC:], C)][n]

        w_raw = y_flat[:, 0:CC * 3 * C].rearrange("p (c n) -> p c n", c=CC)

        @block.sync
        def _(sp):
            give_head_start(sp, "sp")
            for i in range(3):
                sp.dma_start(w_raw[:, :, i * C:(i + 1) * C], wT_d[:, :, i * C:(i + 1) * C]).then_inc(S(f"w{i}_ld"), 16)
                if i == 0:
                    sp.dma_start(at_raw[:], d["adapterT"].rearrange("(c p) j -> p c j", p=P)).then_inc(S("c_ld"), 16)
                    sp.dma_start(cs[:], d["cos_sin"]).then_inc(S("c_ld"), 16)
                    sp.dma_start(ident[:], d["ident"]).then_inc(S("c_ld"), 16)
                    sp.dma_start(akm[:], d["akm"]).then_inc(S("c_ld"), 16)
                    sp.dma_start(avm[:], d["avm"]).then_inc(S("c_ld"), 16)
                    sp.dma_start(cmask[:], d["cmask"]).then_inc(S("c_ld"), 16)
                    sp.dma_start(gate[:], d["gating"].partition_broadcast(P)).then_inc(S("c_ld"), 16)

            def load_x(b, u, tau):
                col = b * T + u * TT if isinstance(b, int) else sp.snap(b * T + u * TT)
                for hf in range(2):
                    at(sp, "xh", 2 * tau + hf, apart=True)
                    at(sp, "xl", 2 * tau + hf, apart=True)
                    sp.dma_start(xs[:], xT_d[:, 2 * hf:2 * hf + 2, bass.ds(col, TT)]).then_inc(S("x_ld"), 16)

            def store_unit(b, u, tau, j):
                n = 4 * tau + j
                dst = (q_parts if j < 2 else k_parts)[bass.ds(b * H + (j % 2) * 16, 16)]
                at(sp, "p3", n + 1)
                for r in range(PARTS):
                    for hf in range(2):
                        sp.dma_start(dst[:, r, 8 * hf:8 * hf + 8, u * TT:(u + 1) * TT],
                                     part[j % 2][:, r, hf, :]).then_inc(S(f"pst{j % 2}"), 16)

            load_x(0, 0, 0)
            with sp.Fori(0, NB) as b:
                for u in range(NTT):
                    tau = NTT * b + u
                    if u == 0:
                        load_x(b, 1, tau + 1)
                        for j in range(NU):
                            store_unit(b, u, tau, j)
                    else:
                        load_x(NB - 1 - b, 0, tau + 1)
                        for j in range(NU):
                            store_unit(b, u, tau, j)

            def load_group(gr):
                if not (gr.fixed and gr.g < 3):
                    at(sp, "sc", HG * QT * (gr.g - 2))
                for dst, src, pick in ((qs[gr.m], q_parts, 0), (ks[gr.m], k_parts, 1)):
                    for r, n, p0 in runs(pick):
                        sp.dma_start(dst[HD * r:HD * (r + n), :, :],
                                     src[bass.ds(gr.g * HG, HG), p0:p0 + n].rearrange("h s d t -> (s d) h t")
                                     ).then_inc(S(f"grp{gr.m}"), 16)

            def store_max(gr, use):
                at(sp, "mr", use + 1)
                sp.dma_start(qs[gr.m][KR:KX].rearrange("s h (q t) -> s (h q) t", t=P), mrow[gr.m][:]
                             ).then_inc(S(f"mrow{gr.m}"), 16)

            for n in range(2):
                at(sp, f"pst{n}", 16 * 6 * TILES * 2)
            sp.nop().then_inc(S("boundary_b"), 1)
            at(sp, "boundary_b", 5)
            load_group(Group(0, 0, 0))
            load_group(Group(1, 1, 0))

            def sp_group(gr):
                if gr.has(2):
                    load_group(gr.plus(2))
                for it in items(gr)[0]:
                    if it[0] == "rows":
                        store_max(gr.plus(1), use_of(gr, it[2])[0])

            store_max(Group(0, 0, 0), NMX)
            drive(sp, sp_group)

            at(sp, "boundary_c", 4)
            sp.dma_start(bias[:], d["base_b"].partition_broadcast(P)).then_inc(S("cc_ld"), 16)
            sp.dma_start(rev[:], d["rev"]).then_inc(S("cc_ld"), 16)
            for n, (name, k0) in enumerate(CW):
                if n >= 2:
                    at(sp, "cwh", n - 1)
                    at(sp, "cwl", n - 1)
                src = d[name].rearrange("(c p) n -> p c n", p=P)[:, k0:k0 + CC]
                sp.dma_start(wst[n % 2][:, :, 0:cw_dst(n)[2]], src).then_inc(S(f"cw{n % 2}_ld"), 16)

            x_d, o_d = d["x"], d["out"]

            def load_xin(t, m):
                at(sp, "x1", t - 1)
                sp.dma_start(xin[m][:], x_d[bass.ds(t * P, P), :]).then_inc(S(f"xin{m}"), 16)

            def store_out(t, m):
                at(sp, "fin", t + 1)
                sp.dma_start(o_d[bass.ds(t * P, P), :], outb[m][:]).then_inc(S(f"ost{m}"), 16)

            load_xin(0, 0)

            def sp_c(j, m):
                if not isinstance(j, int) or j + 1 < NTC:
                    load_xin(j + 1, 1 - m)
                if not isinstance(j, int) or j >= 2:
                    store_out(j - 2, m)

            drive_tiles(sp, sp_c)
            for m in range(2):
                at(sp, f"ost{m}", 16 * NTC // 2)

        @block.gpsimd
        def _(gp):
            give_head_start(gp, "gp")
            def remainders(tau, j):
                n = 4 * tau + j
                at(gp, "p1", n + 1)
                at(gp, "p3", n)
                gp.tensor_tensor(rem[:], rope[j % 2][:], part[j % 2][:, 0], ALU.subtract).then_inc(S("rem"), 1)
                at(gp, "p2", n + 1)
                at(gp, "rem", n + 1)
                gp.tensor_tensor(part[j % 2][:, 2], rem[:], part[j % 2][:, 1], ALU.subtract).then_inc(S("p3"), 1)

            with gp.Fori(0, NB) as b:
                for u in range(NTT):
                    for j in range(NU):
                        remainders(NTT * b + u, j)
            at(gp, "p3", 4 * TILES)
            gp.nop().then_inc(S("boundary_b"), 1)
            at(gp, "boundary_b", 5)
            for i in range(3):
                gp.memset(vb[i][:, :, :, HD:HD + 1], 1.0).then_inc(S("vset"), 1)
                gp.memset(vb[i][:, :, :, HD + 1:VW], 0.0).then_inc(S("vset"), 1)
            for i in range(3):
                at(gp, "vset", 6 + i)
                gp.memset(ks[i][KR:KX], 1.0).then_inc(S("vset"), 1)

            def add_heads(gr, i, use):
                q0, nq = NORM[i]
                at(gp, "mr", use + 1)
                ydst = y_all[:, bass.ds(gr.g, 1), q0:q0 + nq].rearrange("p a q n -> p (a q n)")
                gp.tensor_tensor(ydst, ydst, ynew[:, q0:q0 + nq].rearrange("p q h e -> p (q h e)"),
                                 ALU.add).then_inc(S("yadd"), 1)

            def gp_group(gr):
                for kb in range(QT):
                    if kb in (5, 6, 7) and gr.has(-1):
                        off, = [x[2] for x in items(gr)[0] if x[:2] == ("norm", kb - 5)]
                        add_heads(gr.plus(-1), kb - 5, use_of(gr, off)[0])
                    at(gp, "ex", HG * (QT * gr.g + kb + 1), apart=True)
                    blk = pt[(QT * gr.m + kb) % 3][:, :, kb * P:(kb + 1) * P]
                    gp.affine_select(out=blk, in_=blk, compare_op=ALU.is_ge, fill=0.0, base=0,
                                     pattern=[[0, HG], [1, P]], channel_multiplier=-1).then_inc(S("dg"), 1)

            drive(gp, gp_group)
            for i in range(len(NORM)):
                add_heads(Group(G - 1, (G - 1) % 3, (G - 1) // 3), i, USE0[G] + i)
            at(gp, "dg", 8 * G)
            at(gp, "yadd", len(NORM) * G)
            gp.nop().then_inc(S("boundary_c"), 1)
            at(gp, "boundary_c", 4)
            at(gp, "cc_ld", 32)

            def add_bias(t, m):
                at(gp, "x1", t + 1)
                at(gp, "fin", t - 1)
                gp.tensor_tensor(xb[m][:], x1[m][:], bias[:], ALU.add).then_inc(S("xb"), 1)

            def expand(t, m):
                at(gp, "comb", t + 1)
                at(gp, "hr", t + 1)
                at(gp, "tg", t - 1)
                gp.tensor_tensor(gbuf[m][:], comb[m][:].unsqueeze(2).to_broadcast([P, E, R]),
                                 hr[m][:].unsqueeze(1).to_broadcast([P, E, R]), ALU.mult).then_inc(S("g"), 1)

            def gp_c(j, m):
                if not isinstance(j, int) or 1 <= j <= NTC:
                    expand(j - 1, 1 - m)
                if not isinstance(j, int) or j < NTC:
                    add_bias(j, m)

            drive_tiles(gp, gp_c)

        @block.scalar
        def _(act):
            give_head_start(act, "act")
            for i in range(3):
                at(act, f"w{i}_ld", 16)
                act.copy(wh[:, :, i * C:(i + 1) * C], w_raw[:, :, i * C:(i + 1) * C]).then_inc(S("wh"), 1)
                if i == 0:
                    at(act, "c_ld", 16 * 7)
                    act.copy(ath[:].rearrange("p c (h j) -> p c h j", j=J),
                             at_raw[:].unsqueeze(2).to_broadcast([P, CC, 8, J])).then_inc(S("ath"), 1)

            def x_high(tau, m):
                for hf in range(2):
                    at(act, "x_ld", 16 * (2 * tau + hf + 1))
                    at(act, "uf", NU * (tau - 1))
                    act.copy(xh[m][:, 2 * hf:2 * hf + 2], xs[:]).then_inc(S("xh"), 1)

            def first(tau, j):
                n = 4 * tau + j
                at(act, "ro", n + 1)
                at(act, f"pst{j % 2}", 16 * 6 * (2 * tau + j // 2))
                act.copy(part[j % 2][:, 0], rope[j % 2][:]).then_inc(S("p1"), 1)

            def second(tau, j):
                at(act, "rem", 4 * tau + j + 1)
                act.copy(part[j % 2][:, 1], rem[:]).then_inc(S("p2"), 1)

            def evac(tau, w, out, src):
                at(act, "vf", NV * tau + w + 1)
                act.copy(out, src).then_inc(S("vr"), 1)

            def exp_a(tau, a_):
                m = 4 * tau + a_
                at(act, "asub", m + 1)
                act.activation(asb[a_ % 2][:], asb[a_ % 2][:], ACT.Exp, scale=float(C) ** -0.5).then_inc(S("aex"), 1)

            x_high(0, 0)

            with act.Fori(0, NB) as b:
                for u in range(NTT):
                    tau = NTT * b + u

                    def v_out(a_):
                        return v_all[:, bass.ds(b * GB, GB), u * 4 + a_, :]

                    def y_out(a_):
                        return y_all[:, bass.ds(b * GB, GB), u * 4 + a_, :]

                    def vb_(w):
                        return half(4 + w % 2)

                    first(tau, 0)
                    evac(tau, 0, v_out(0), vb_(0).rearrange("p (g n) -> p g n", g=GB))
                    second(tau, 0)
                    evac(tau, 1, v_out(1), vb_(1).rearrange("p (g n) -> p g n", g=GB))
                    first(tau, 1)
                    evac(tau, 2, v_out(2), vb_(2).rearrange("p (g n) -> p g n", g=GB))
                    evac(tau, 3, v_out(3), vb_(3).rearrange("p (g n) -> p g n", g=GB))
                    second(tau, 1)
                    for a_ in range(4):
                        exp_a(tau, a_)
                    x_high(tau + 1, 1 - u)
                    evac(tau, 4, pat[0][:], vb_(4)[0:80].rearrange("p (g n) -> p g n", g=4))
                    evac(tau, 5, pat[1][:], vb_(5)[0:80].rearrange("p (g n) -> p g n", g=4))
                    first(tau, 2)
                    evac(tau, 6, y_out(0), vb_(6).rearrange("p (g n) -> p g n", g=GB))
                    evac(tau, 7, y_out(1), vb_(7).rearrange("p (g n) -> p g n", g=GB))
                    second(tau, 2)
                    evac(tau, 8, pat[0][:], vb_(8)[0:80].rearrange("p (g n) -> p g n", g=4))
                    evac(tau, 9, pat[1][:], vb_(9)[0:80].rearrange("p (g n) -> p g n", g=4))
                    first(tau, 3)
                    evac(tau, 10, y_out(2), vb_(10).rearrange("p (g n) -> p g n", g=GB))
                    evac(tau, 11, y_out(3), vb_(11).rearrange("p (g n) -> p g n", g=GB))
                    second(tau, 3)
            at(act, "p2", 4 * TILES)
            act.nop().then_inc(S("boundary_b"), 1)
            at(act, "boundary_b", 5)

            at(act, "vset", 9)

            def build_v(gr):
                if not (gr.fixed and gr.g < 3):
                    at(act, "pv", QT * (gr.g - 2))
                act.copy(vb[gr.m][:, :, :, 0:HD],
                         v_all[:, bass.ds(gr.g, 1)].rearrange("p a q (h e) -> p (a q) h e", e=HD)).then_inc(S("vb"), 1)

            def evac_y(gr):
                at(act, "pv", QT * (gr.g + 1))
                if gr.has(-1):
                    at(act, "mf", norm_end(gr))
                act.copy(yts[:], bank[3][:]).then_inc(S("yts"), 1)

            def act_group(gr):
                for kb in range(QT):
                    st = QT * gr.g + kb
                    if not (gr.fixed and st < 3):
                        at(act, "pv", st - 2)
                    for h in range(HG):
                        at(act, "sc", HG * st + h + 1)
                        act.activation(pt[(QT * gr.m + kb) % 3][:, h, kb * P:T], bank[h % 2][:, 0:T - kb * P], ACT.Exp,
                                       scale=float(HD) ** -0.5).then_inc(S("ex"), 1)
                    if kb == 1 and gr.has(-1):
                        evac_y(gr.plus(-1))
                    if kb == 3 and gr.has(1):
                        build_v(gr.plus(1))

            build_v(Group(0, 0, 0))
            drive(act, act_group)
            evac_y(Group(G - 1, (G - 1) % 3, (G - 1) // 3))
            at(act, "yts", G)
            act.nop().then_inc(S("boundary_c"), 1)
            at(act, "boundary_c", 4)

            for n, (name, k0) in enumerate(CW):
                hi, lo, w = cw_dst(n)
                at(act, f"cw{n % 2}_ld", 16 * (n // 2 + 1))
                act.copy(hi, wst[n % 2][:, :, 0:w]).then_inc(S("cwh"), 1)

            def tile_y(t, m):
                at(act, "ty", t - 1)
                bb, qt = t >> 3, t & 7
                if not isinstance(t, int):
                    bb = nc.s_assert_within(bb, 0, NB - 1, skip_runtime_bounds_check_because="t < NB * QT")
                act.copy(ytile[m][:].rearrange("p (g n) -> p g n", g=GB),
                         y_all[:, bass.ds(bb * GB, GB), bass.ds(qt, 1), :].rearrange("p g a n -> p g (a n)")
                         ).then_inc(S("yt"), 1)

            def hi_x(t, m):
                at(act, "tx", t + 1)
                act.copy(xth[m][:].rearrange("p c n -> p (c n)"), half(0)).then_inc(S("xth"), 1)

            def hi_g(t):
                at(act, "tg", t + 1)
                act.copy(gth[:].rearrange("p c n -> p (c n)"), bank[3][:]).then_inc(S("gth"), 1)

            def router_exp(t, m):
                at(act, "nmax", t + 1)
                act.copy(hr[m][:], half(3)[:, 0:R]).then_inc(S("hr"), 1)
                act.activation(ex[m][:], half(3)[:, R:R + E], ACT.Exp, bias=sm[:, 8 + 2 * m:9 + 2 * m], scale=1.0,
                               accum_out=sm[:, 9 + 2 * m:10 + 2 * m]).then_inc(S("rex"), 1)

            def hi_y(t, m):
                at(act, "ty", t + 1)
                act.copy(yth[m][:].rearrange("p c n -> p (c n)"), half(1)).then_inc(S("yth"), 1)

            tile_y(0, 0)
            hi_y(0, 0)

            def act_c(j, m):
                sure = not isinstance(j, int)
                if sure or j + 1 < NTC:
                    tile_y(j + 1, 1 - m)
                if sure or 1 <= j <= NTC:
                    hi_x(j - 1, 1 - m)
                if sure or 2 <= j:
                    hi_g(j - 2)
                if sure or 1 <= j <= NTC:
                    router_exp(j - 1, 1 - m)
                if sure or j + 1 < NTC:
                    hi_y(j + 1, 1 - m)

            drive_tiles(act, act_c)

        @block.vector
        def _(ve):
            give_head_start(ve, "ve")
            for i in range(3):
                at(ve, "wh", i + 1)
                ve.tensor_tensor(wl[:, :, i * C:(i + 1) * C], w_raw[:, :, i * C:(i + 1) * C],
                                 wh[:, :, i * C:(i + 1) * C], ALU.subtract).then_inc(S("wl"), 1)
                if i == 0:
                    at(ve, "ath", 1)
                    ve.tensor_tensor(atl[:].rearrange("p c (h j) -> p c h j", j=J),
                                     at_raw[:].unsqueeze(2).to_broadcast([P, CC, 8, J]),
                                     ath[:].rearrange("p c (h j) -> p c h j", j=J), ALU.subtract).then_inc(S("atl"), 1)
                    ve.tensor_copy(identb[:], ident[:]).then_inc(S("idb"), 1)

            def x_low(tau, m):
                for hf in range(2):
                    at(ve, "xh", 2 * tau + hf + 1)
                    ve.tensor_tensor(xl[m][:, 2 * hf:2 * hf + 2], xs[:], xh[m][:, 2 * hf:2 * hf + 2],
                                     ALU.subtract).then_inc(S("xl"), 1)

            x_low(0, 0)
            at(ve, "akf", 1)
            ak_sb = rope[0][0:80, 0, :]
            ve.tensor_copy(ak_sb, half(6)[0:80]).then_inc(S("aks"), 1)
            at(ve, "avf", 1)
            ve.tensor_tensor(avbd[:].rearrange("p a (h e) -> p a h e", e=HD),
                             half(7)[0:80].rearrange("p (a h e) -> p a h e", a=4, e=HD),
                             avm[:].unsqueeze(1).unsqueeze(3).to_broadcast([80, 4, 8, HD]), ALU.mult).then_inc(S("avbd"), 1)
            at(ve, "akt", 1)
            for hg in range(2):
                for hf in range(2):
                    i = 2 * hg + hf
                    ve.tensor_tensor(akbd[:, hg, hf],
                                     akm[:].unsqueeze(2).to_broadcast([P, 16, J]),
                                     half(6)[:, 80 * i:80 * i + J].unsqueeze(1).to_broadcast([P, 16, J]),
                                     ALU.mult).then_inc(S("akbd"), 1)

            def rotate(tau, u, j):
                n = 4 * tau + j
                at(ve, "uf", n + 1)
                a_, b_ = half(2 * (j % 2)), half(2 * (j % 2) + 1)
                cos, sin = (cs[:, i, u * TT:(u + 1) * TT] for i in range(2))
                ro = rope[j % 2]
                at(ve, "rem", n - 1)
                if j >= 2:
                    at(ve, "as", 4 * tau + 4)
                at(ve, "ro", n)
                ve.tensor_tensor(ro[:, 0], a_, cos, ALU.mult).then_inc(S("tm"), 1)
                ve.tensor_tensor(rtmp[0][:], b_, sin, ALU.mult).then_inc(S("tm"), 1)
                ve.tensor_tensor(ro[:, 1], b_, cos, ALU.mult).then_inc(S("tm"), 1)
                ve.tensor_tensor(rtmp[1][:], a_, sin, ALU.mult).then_inc(S("tm"), 1)
                at(ve, "tm", 4 * (n + 1))
                ve.tensor_tensor(ro[:, 0], ro[:, 0], rtmp[0][:], ALU.subtract)
                ve.tensor_tensor(ro[:, 1], ro[:, 1], rtmp[1][:], ALU.add).then_inc(S("ro"), 1)

            def soft_a(tau, a_):
                m = 4 * tau + a_
                at(ve, "as", m + 1)
                sc = half(6 + a_ % 2)[:, 0:H * J].rearrange("p (h j) -> p h j", j=J)
                ve.tensor_reduce(asum[:, 0], sc, AX.X, ALU.max).then_inc(S("ad"), 1)
                at(ve, "ad", 5 * m + 1)
                ve.tensor_tensor(asb[a_ % 2][:], sc, asum[:, 0].unsqueeze(2).to_broadcast([P, H, J]),
                                 ALU.subtract).then_inc(S("asub"), 1)
                at(ve, "aex", m + 1)
                ve.tensor_reduce(asum[:, 1], asb[a_ % 2][:], AX.X, ALU.add).then_inc(S("ad"), 1)
                at(ve, "ad", 5 * m + 2)
                ve.reciprocal(asum[:, 2], asum[:, 1]).then_inc(S("ad"), 1)
                at(ve, "ad", 5 * m + 3)
                ve.tensor_scalar(asum[:, 3], asum[:, 2], gate[:, 0:1], None, ALU.mult).then_inc(S("ad"), 1)
                at(ve, "ad", 5 * m + 4)
                ve.tensor_tensor(pa[a_][:], asb[a_ % 2][:], asum[:, 3].unsqueeze(2).to_broadcast([P, H, J]),
                                 ALU.mult).then_inc(S("ad"), 1)

            with ve.Fori(0, NB) as b:
                for u in range(NTT):
                    tau = NTT * b + u
                    rotate(tau, u, 0)
                    rotate(tau, u, 1)
                    for a_ in range(4):
                        soft_a(tau, a_)
                    x_low(tau + 1, 1 - u)
                    rotate(tau, u, 2)
                    rotate(tau, u, 3)
            at(ve, "ro", 4 * TILES)
            at(ve, "xl", 2 * TILES + 2)
            ve.nop().then_inc(S("boundary_b"), 1)
            at(ve, "boundary_b", 5)

            for m in range(3):
                ve.memset(mx[m][:], NEG).then_inc(S("mset"), 1)
            at(ve, "mset", 3)

            def max_bank(gr, w, use, bk):
                h, pieces = w // NMB, MAX_BANKS[w % NMB]
                at(ve, "mf", use + 1, apart=True)
                src, m = half(4 + bk), gr.m
                col, last = 0, None
                for qt, k0, nk in pieces:
                    dg = k0 + nk == qt + 1
                    full = nk - dg
                    if full:
                        last = ve.tensor_reduce(mx[m][:, 1 + (k0 > 0), h, qt:qt + 1], src[:, col:col + full * P],
                                                AX.X, ALU.max)
                    if dg:
                        blk = src[:, col + full * P:col + nk * P]
                        last = ve.tensor_tensor_reduce(blk, blk, cmask[:], 1.0, NEG, ALU.add, ALU.max, mx[m][:, 0, h, qt:qt + 1])
                    col += nk * P
                last.then_inc(S("mr"), 1)

            def max_rows(gr, use):
                g = gr.g
                at(ve, "mr", use)
                ve.tensor_reduce(mall[:], mx[gr.m][:].rearrange("p s h q -> p (h q) s"), AX.X, ALU.max
                                 ).then_inc(S("mall"), 1)
                at(ve, "mall", g + 1)
                ve.tensor_scalar(mneg[:, 0], mall[:], -1.0, None, ALU.mult).then_inc(S("mn0"), 1)
                at(ve, "mn0", g + 1)
                ve.scalar_tensor_tensor(out=mneg[:, 1], in0=mall[:], scalar=-1.0, in1=mneg[:, 0],
                                        op0=ALU.mult, op1=ALU.subtract).then_inc(S("mn"), 1)

            def copy_rows(gr, use, bk):
                at(ve, "mf", use + 1)
                ve.tensor_copy(mrow[gr.m][:], half(4 + bk).bitcast(BF16)[0:2 * HG * QT, 0:P]).then_inc(S("mr"), 1)

            def normalise(gr, i, use, bk):
                q0, nq = NORM[i]
                at(ve, "mf", use + 1)
                src = half(4 + bk)[:, 0:nq * P].rearrange("p (q h e) -> p q h e", q=nq, h=HG)
                k = len(NORM) * gr.g + i
                ve.reciprocal(rden[:, q0:q0 + nq], src[:, :, :, HD:HD + 1].rearrange("p q h e -> p q (h e)")
                              ).then_inc(S("nm"), 1)
                at(ve, "nm", k + 1)
                at(ve, "yadd", k - len(NORM) + 1)
                ve.tensor_tensor(ynew[:, q0:q0 + nq], src[:, :, :, 0:HD],
                                 rden[:, q0:q0 + nq].unsqueeze(3).to_broadcast([P, nq, HG, HD]), ALU.mult).then_inc(S("mr"), 1)

            def ve_group(gr):
                for it in items(gr)[0]:
                    if it[0] == "max":
                        max_bank(gr.plus(it[1]), it[2], *use_of(gr, it[3]))
                    elif it[0] == "calc":
                        max_rows(gr.plus(1), use_of(gr, it[2])[0])
                    elif it[0] == "rows":
                        copy_rows(gr.plus(1), *use_of(gr, it[2]))
                    elif it[0] == "norm":
                        normalise(gr.plus(-1), it[1], *use_of(gr, it[2]))

            g0, g1, gz = Group(0, 0, 0), Group(1, 1, 0), Group(G - 1, (G - 1) % 3, (G - 1) // 3)
            for w in range(NMX):
                max_bank(g0, w, w, w % 2)
            max_rows(g0, NMX)
            copy_rows(g0, NMX, NMX % 2)
            for w in range(LEAD):
                max_bank(g1, w, NMX + 1 + w, (NMX + 1 + w) % 2)
            drive(ve, ve_group)
            for i in range(len(NORM)):
                normalise(gz, i, USE0[G] + i, (USE0[G] + i) % 2)
            at(ve, "mr", PSM_TOTAL)
            ve.nop().then_inc(S("boundary_c"), 1)
            at(ve, "boundary_c", 4)

            for n, (name, k0) in enumerate(CW):
                hi, lo, w = cw_dst(n)
                at(ve, "cwh", n + 1)
                ve.tensor_tensor(lo, wst[n % 2][:, :, 0:w], hi, ALU.subtract).then_inc(S("cwl"), 1)
            at(ve, "cc_ld", 32)

            def lo_y(t, m):
                at(ve, "yth", t + 1)
                ve.tensor_tensor(ytl[m][:].rearrange("p c n -> p (c n)"), half(1), yth[m][:].rearrange("p c n -> p (c n)"),
                                 ALU.subtract).then_inc(S("ytl"), 1)

            def lo_x(t, m):
                at(ve, "xth", t + 1)
                ve.tensor_tensor(xtl[m][:].rearrange("p c n -> p (c n)"), half(0), xth[m][:].rearrange("p c n -> p (c n)"),
                                 ALU.subtract).then_inc(S("xtl"), 1)

            def lo_g(t):
                at(ve, "gth", t + 1)
                ve.tensor_tensor(gtl[:].rearrange("p c n -> p (c n)"), bank[3][:], gth[:].rearrange("p c n -> p (c n)"),
                                 ALU.subtract).then_inc(S("gtl"), 1)

            def norm_to(t, src, out, o, name, done):
                k = [NORM_STEPS * t]

                def link(ins):
                    ins.then_inc(S(name), 1)
                    k[0] = k[0] + 1
                    at(ve, name, k[0], apart=True)

                v, y, u = (sm[:, o + 12 + i:o + 13 + i] for i in range(3))
                link(ve.bn_stats(sm[:, o:o + 6], src))
                link(ve.bn_aggr(sm[:, o + 10:o + 12], sm[:, o:o + 6]))
                link(ve.tensor_scalar(v, sm[:, o + 11:o + 12], EPS, None, ALU.add))
                link(ve.tensor_scalar(y.bitcast(I32), v.bitcast(I32), -0.5, float(0x5F3759DF), ALU.mult, ALU.add))
                for _ in range(NEWTON):
                    link(ve.scalar_tensor_tensor(out=u, in0=y, scalar=v, in1=y, op0=ALU.mult, op1=ALU.mult))
                    link(ve.tensor_scalar(u, u, -0.5, 1.5, ALU.mult, ALU.add))
                    link(ve.tensor_tensor(y, y, u, ALU.mult))
                ve.tensor_scalar(out, src, sm[:, o + 10:o + 11], y, ALU.subtract, ALU.mult).then_inc(S(done), 1)

            def ln1(t, m):
                at(ve, "proj", t + 1)
                at(ve, f"xin{m}", 16 * ((t >> 1) + 1) if not isinstance(t, int) else 16 * (t // 2 + 1))
                at(ve, "xb", t - 1)
                at(ve, "tx", t - 1)
                ve.tensor_tensor(xin[m][:], xin[m][:], half(2), ALU.add).then_inc(S("xs_"), 1)
                at(ve, "xs_", t + 1)
                norm_to(t, xin[m][:], x1[m][:], 16, "n1", "x1")

            def route(t, m):
                o = 2 * m
                at(ve, "ar", t + 1, apart=True)
                top = sm[:, 48:56]
                ve.max(top, half(3)[:, R:R + E]).then_inc(S("rt"), 1)
                k = 13 * t
                step = [k + 1]

                def link(ins):
                    ins.then_inc(S("rt"), 1)
                    step[0] = step[0] + 1

                def sync():
                    at(ve, "rt", step[0])
                sync()
                ve.tensor_scalar(sm[:, 8 + o:9 + o], top[:, 0:1], -1.0, None, ALU.mult).then_inc(S("nmax"), 1)
                at(ve, "rex", t + 1, apart=True)
                e_ = ex[m][:]
                big = sm[:, 56:64]
                link(ve.max(big, e_))
                sync()
                link(ve.scalar_tensor_tensor(out=rt[:, 0], in0=e_, scalar=big[:, 0:1], in1=rev[:],
                                             op0=ALU.is_equal, op1=ALU.mult))
                sync()
                link(ve.tensor_reduce(sm[:, 64:65], rt[:, 0], AX.X, ALU.max))
                sync()
                link(ve.tensor_scalar(rt[:, 1], rt[:, 0], sm[:, 64:65], None, ALU.is_equal))
                sync()
                link(ve.scalar_tensor_tensor(out=rt[:, 2], in0=rt[:, 1], scalar=-2.0, in1=e_, op0=ALU.mult, op1=ALU.add))
                sync()
                link(ve.scalar_tensor_tensor(out=rt[:, 3], in0=rt[:, 2], scalar=big[:, 1:2], in1=rev[:],
                                             op0=ALU.is_equal, op1=ALU.mult))
                sync()
                link(ve.tensor_reduce(sm[:, 65:66], rt[:, 3], AX.X, ALU.max))
                sync()
                link(ve.scalar_tensor_tensor(out=rt[:, 4], in0=rt[:, 3], scalar=sm[:, 65:66], in1=rt[:, 1],
                                             op0=ALU.is_equal, op1=ALU.add))
                sync()
                link(ve.tensor_tensor(rt[:, 5], rt[:, 4], e_, ALU.mult))
                link(ve.tensor_tensor(sm[:, 66:67], big[:, 0:1], big[:, 1:2], ALU.add))
                sync()
                link(ve.scalar_tensor_tensor(out=sm[:, 67:68], in0=sm[:, 9 + o:10 + o], scalar=1e-6, in1=sm[:, 66:67],
                                             op0=ALU.mult, op1=ALU.add))
                sync()
                link(ve.reciprocal(sm[:, 68:69], sm[:, 67:68]))
                sync()
                at(ve, "g", t - 1)
                ve.tensor_scalar(comb[m][:], rt[:, 5], sm[:, 68:69], 0.5, ALU.mult, ALU.mult).then_inc(S("comb"), 1)
                if isinstance(t, int):
                    assert step[0] == 13 * (t + 1)

            def ln2(t, m):
                at(ve, "ff", t + 1)
                at(ve, "xb", t + 1)
                ve.tensor_tensor(xb[m][:], xb[m][:], half(4 + m), ALU.add).then_inc(S("fs"), 1)
                at(ve, "fs", t + 1)
                if not (isinstance(t, int) and t < 2):
                    at(ve, f"ost{m}", 16 * (t >> 1))
                norm_to(t, xb[m][:], outb[m][:], 32, "n2", "fin")

            lo_y(0, 0)

            def ve_c(j, m):
                sure = not isinstance(j, int)
                if sure or 1 <= j <= NTC:
                    lo_x(j - 1, 1 - m)
                if sure or j >= 2:
                    lo_g(j - 2)
                if sure or j < NTC:
                    ln1(j, m)
                if sure or 1 <= j <= NTC:
                    route(j - 1, 1 - m)
                if sure or j + 1 < NTC:
                    lo_y(j + 1, 1 - m)
                if sure or j >= 2:
                    ln2(j - 2, m)

            drive_tiles(ve, ve_c)

        @block.tensor
        def _(pe):
            give_head_start(pe, "pe")
            at(pe, "atl", 1)
            for i, (w0, bk) in enumerate(((1, 6), (2, 7))):
                at(pe, "wl", w0 + 1)
                for c_ in range(CC):
                    last = three(pe, half(bk)[0:80], ath[:, c_], atl[:, c_], wh[:, c_, w0 * C:(w0 + 1) * C],
                                 wl[:, c_, w0 * C:(w0 + 1) * C], c_ == 0, c_ == CC - 1)
                last.then_inc(S(("akf", "avf")[i]), 1)
            at(pe, "aks", 1)
            for i in range(4):
                last = pe.transpose(half(6)[:, 80 * i:80 * i + 80], rope[0][0:80, 0, i * P:(i + 1) * P], ident[0:80, 0:80])
            last.then_inc(S("akt"), 1)

            def unit_half(tau, m, j, hf):
                n = 4 * tau + j
                if hf == 0:
                    at(pe, "tm", 4 * (n - 1))
                o = j * 256 + hf * P
                for c_ in range(CC):
                    last = three(pe, half(2 * (j % 2) + hf), wh[:, c_, o:o + P], wl[:, c_, o:o + P],
                                 xh[m][:, c_], xl[m][:, c_], c_ == 0, c_ == CC - 1)
                if hf == 1:
                    last.then_inc(S("uf"), 1)
                return last

            def v_use(tau, w):
                at(pe, "vr", NV * tau + w - 1)
                return half(4 + w % 2)

            def values(tau, m, a_):
                out = v_use(tau, a_)
                for c_ in range(CC):
                    last = three(pe, out, xh[m][:, c_, a_ * P:(a_ + 1) * P], xl[m][:, c_, a_ * P:(a_ + 1) * P],
                                 wh[:, c_, 2 * C:3 * C], wl[:, c_, 2 * C:3 * C], c_ == 0, c_ == CC - 1)
                last.then_inc(S("vf"), 1)

            def a_scores(tau, a_):
                m = 4 * tau + a_
                at(pe, "ro", 4 * tau + 2)
                at(pe, "asub", m - 1)
                for hg in range(2):
                    for hf in range(2):
                        last = pe.matmul(half(6 + a_ % 2)[:, hg * 160:hg * 160 + 160], rope[hg][:, hf, a_ * P:(a_ + 1) * P],
                                         akbd[:, hg, hf].rearrange("p h j -> p (h j)"), start=(hf == 0), stop=(hf == 1))
                last.then_inc(S("as"), 1)

            def a_trans(tau, a_, w):
                out = v_use(tau, w)
                at(pe, "ad", 5 * (4 * tau + a_ + 1))
                src = pa[a_][:].rearrange("p h j -> p (h j)")
                for i in range(4):
                    last = pe.transpose(out[0:80, i * P:(i + 1) * P], src[:, 80 * i:80 * i + 80], ident[:])
                last.then_inc(S("vf"), 1)

            def a_out(tau, a_, w):
                out = v_use(tau, w)
                at(pe, "vr", NV * tau + w - 1)
                for i in range(4):
                    last = pe.matmul(out[:, i * P:(i + 1) * P], pat[a_ % 2][:, i], avbd[:, i], start=True, stop=True)
                last.then_inc(S("vf"), 1)

            at(pe, "wl", 3)
            at(pe, "akbd", 4)
            with pe.Fori(0, NB) as b:
                for u in range(NTT):
                    tau = NTT * b + u
                    at(pe, "xl", 2 * (tau + 1))
                    for j in range(2):
                        unit_half(tau, u, j, 0)
                        unit_half(tau, u, j, 1)
                    for a_ in range(4):
                        values(tau, u, a_)
                    for a_ in range(4):
                        a_scores(tau, a_)
                    unit_half(tau, u, 2, 0)
                    unit_half(tau, u, 2, 1)
                    a_trans(tau, 0, 4)
                    a_trans(tau, 1, 5)
                    unit_half(tau, u, 3, 0)
                    a_out(tau, 0, 6)
                    a_out(tau, 1, 7)
                    a_trans(tau, 2, 8)
                    a_trans(tau, 3, 9)
                    unit_half(tau, u, 3, 1)
                    a_out(tau, 2, 10)
                    a_out(tau, 3, 11)
            at(pe, "vf", NV * TILES)
            pe.nop().then_inc(S("boundary_b"), 1)
            at(pe, "boundary_b", 5)
            at(pe, "vset", 9)

            def free_bank(use, apart=False):
                at(pe, "mr", use - 1, apart)

            def score(gr, kb, h):
                m, n = gr.m, HG * (QT * gr.g + kb) + h
                if kb == 0 and h == 0:
                    at(pe, f"mrow{m}", 16 * (gr.v + 1))
                if not (gr.fixed and n < 2):
                    at(pe, "ex", n - 1)
                width = T - kb * P
                for c0 in range(0, width, 512):
                    w = min(512, width - c0)
                    last = pe.matmul(bank[h % 2][:, c0:c0 + w], ks[m][0:KX, h, kb * P:(kb + 1) * P],
                                     qs[m][0:KX, h, kb * P + c0:kb * P + c0 + w], start=True, stop=True)
                last.then_inc(S("sc"), 1)

            def max_scores(gr, w, use, bk):
                h, m = w // NMB, gr.m
                if w == 0:
                    at(pe, f"grp{m}", 16 * GROUP_LOADS * (gr.v + 1))
                free_bank(use)
                out, col = half(4 + bk), 0
                for qt, k0, nk in MAX_BANKS[w % NMB]:
                    last = pe.matmul(out[:, col:col + nk * P], qs[m][0:KR, h, qt * P:(qt + 1) * P],
                                     ks[m][0:KR, h, k0 * P:(k0 + nk) * P], start=True, stop=True)
                    col += nk * P
                last.then_inc(S("mf"), 1)

            def trans_rows(gr, use, bk):
                at(pe, "mn", gr.g + 1)
                free_bank(use, apart=True)
                pe.transpose(half(4 + bk).bitcast(BF16)[0:2 * HG * QT, 0:P], mneg[:].rearrange("p s n -> p (s n)"),
                             identb[:]).then_inc(S("mf"), 1)

            def trans_out(gr, i, use, bk):
                q0, nq = NORM[i]
                at(pe, "yts", gr.g + 1)
                free_bank(use)
                for q in range(nq):
                    last = pe.transpose(half(4 + bk)[:, q * P:(q + 1) * P], yts[:, (q0 + q) * P:(q0 + q + 1) * P],
                                        ident[:])
                last.then_inc(S("mf"), 1)

            def weighted(gr, kb, q0, q1, h0, done):
                if kb == 0 and q0 == 0 and h0 == 0:
                    at(pe, "vb", gr.g + 1)
                    at(pe, "yts", gr.g)
                if q0 == kb * P and h0 == 0:
                    at(pe, "dg", QT * gr.g + kb + 1)
                src = pt[(QT * gr.m + kb) % 3]
                for h in (h0, h0 + 1):
                    last = pe.matmul(bank[3][VW * h:VW * h + VW, q0:q1], vb[gr.m][:, kb, h, :],
                                     src[:, h, q0:q1], start=(kb == 0), stop=(kb == q1 // P - 1))
                if done:
                    last.then_inc(S("pv"), 1)

            def pe_group(gr):
                for it in items(gr)[0]:
                    if it[0] == "score":
                        score(gr, it[1], it[2])
                    elif it[0] == "max":
                        max_scores(gr.plus(it[1]), it[2], *use_of(gr, it[3]))
                    elif it[0] == "rows":
                        trans_rows(gr.plus(1), *use_of(gr, it[2]))
                    elif it[0] == "norm":
                        trans_out(gr.plus(-1), it[1], *use_of(gr, it[2]))
                    elif it[0] == "pv":
                        weighted(gr.plus(it[1]), *it[2:])

            g0, g1, gz = Group(0, 0, 0), Group(1, 1, 0), Group(G - 1, (G - 1) % 3, (G - 1) // 3)
            for w in range(NMX):
                max_scores(g0, w, w, w % 2)
            trans_rows(g0, NMX, NMX % 2)
            for w in range(LEAD):
                max_scores(g1, w, NMX + 1 + w, (NMX + 1 + w) % 2)
            drive(pe, pe_group)
            for kb in range(QT - LAG, QT):
                for piece in value_pieces(kb):
                    weighted(gz, kb, *piece)
            for i in range(len(NORM)):
                trans_out(gz, i, USE0[G] + i, (USE0[G] + i) % 2)
            at(pe, "mf", PSM_TOTAL)
            pe.nop().then_inc(S("boundary_c"), 1)
            at(pe, "boundary_c", 4)

            at(pe, "cwl", len(CW))

            def t_y(t, m):
                at(pe, "yt", t + 1)
                at(pe, "ytl", t)
                for c_ in range(CC):
                    last = pe.transpose(half(1)[:, c_ * P:(c_ + 1) * P], ytile[m][:, c_ * P:(c_ + 1) * P], ident[:])
                last.then_inc(S("ty"), 1)

            def proj(t, m):
                at(pe, "ytl", t + 1)
                at(pe, "xs_", t)
                for c_ in range(CC):
                    last = three(pe, half(2), yth[m][:, c_], ytl[m][:, c_], wph[:, c_], wpl[:, c_], c_ == 0, c_ == CC - 1)
                last.then_inc(S("proj"), 1)

            def t_x(t, m):
                at(pe, "x1", t + 1)
                at(pe, "xtl", t)
                for c_ in range(CC):
                    last = pe.transpose(half(0)[:, c_ * P:(c_ + 1) * P], x1[m][:, c_ * P:(c_ + 1) * P], ident[:])
                last.then_inc(S("tx"), 1)

            def t_g(t, m):
                at(pe, "g", t + 1)
                at(pe, "gtl", t)
                gf = gbuf[m][:].rearrange("p e r -> p (e r)")
                for c_ in range(8):
                    last = pe.transpose(bank[3][:, c_ * P:(c_ + 1) * P], gf[:, c_ * P:(c_ + 1) * P], ident[:])
                last.then_inc(S("tg"), 1)

            def ar(t, m):
                at(pe, "xtl", t + 1)
                at(pe, "rex", t)
                at(pe, "hr", t)
                for c_ in range(CC):
                    last = three(pe, half(3)[:, 0:R + E], xth[m][:, c_], xtl[m][:, c_], arh[:, c_], arl[:, c_],
                                 c_ == 0, c_ == CC - 1)
                last.then_inc(S("ar"), 1)

            def base(t, m):
                at(pe, "fs", t - 1)
                for c_ in range(CC):
                    three(pe, half(4 + m), xth[m][:, c_], xtl[m][:, c_], wfh[:, c_], wfl[:, c_], c_ == 0, False)

            def delta(t, m):
                at(pe, "gtl", t + 1)
                for c_ in range(8):
                    last = three(pe, half(4 + m), gth[:, c_], gtl[:, c_], wbh[:, c_], wbl[:, c_], False, c_ == 7)
                last.then_inc(S("ff"), 1)

            t_y(0, 0)

            def pe_c(j, m):
                sure = not isinstance(j, int)
                if sure or 1 <= j <= NTC:
                    t_x(j - 1, 1 - m)
                if sure or j < NTC:
                    proj(j, m)
                if sure or j >= 2:
                    t_g(j - 2, m)
                if sure or 1 <= j <= NTC:
                    ar(j - 1, 1 - m)
                    base(j - 1, 1 - m)
                if sure or j + 1 < NTC:
                    t_y(j + 1, 1 - m)
                if sure or j >= 2:
                    delta(j - 2, m)

            drive_tiles(pe, pe_c)


def constants():
    import numpy as np

    theta = np.float32(1.0) / np.power(np.float32(10000.0), (np.arange(0, HD, 2, dtype=np.float32) / np.float32(HD)))
    angle = np.outer(np.arange(T, dtype=np.float32), theta.astype(np.float32)).astype(np.float32)
    cs = np.stack([np.cos(angle.astype(np.float64)), np.sin(angle.astype(np.float64))]).astype(np.float32)
    p = np.arange(P)
    a = np.arange(8 * J)
    return {
        "cos_sin": np.ascontiguousarray(cs[:, :, p % 8].transpose(2, 0, 1)),
        "ident": np.eye(P, dtype=np.float32),
        "akm": (p[:, None] // 8 == np.arange(16)).astype(np.float32),
        "avm": (a[:, None] // J == np.arange(8)).astype(np.float32),
        "cmask": np.where(p[None, :] <= p[:, None], 0.0, NEG).astype(np.float32),
        "rev": np.ascontiguousarray(np.broadcast_to(np.arange(E, 0, -1, dtype=np.float32), (P, E))),
    }


def kernel(L0_attn_x, L0_attn_w_attn, L0_attn_w_proj, L0_attn_adapter_wte, L0_attn_gating, L0_ffn_base_w,
           L0_ffn_base_b, L0_ffn_A, L0_ffn_B, L0_ffn_router_w):
    import numpy as np
    import concourse.bacc as bacc
    from concourse.bass_utils import run_bass_kernel_spmd

    x = np.asarray(L0_attn_x).reshape(NB * T, C)
    w = np.asarray(L0_attn_w_attn)
    qk = w[:2 * C].reshape(2, 2, 16, 2, 8, C).transpose(0, 1, 3, 2, 4, 5).reshape(2 * C, C)
    arrays = {
        "x": x,
        "xT": x.T,
        "w_attnT": np.concatenate([qk, w[2 * C:]]).T,
        "w_projT": np.asarray(L0_attn_w_proj).T,
        "adapterT": np.asarray(L0_attn_adapter_wte).T,
        "gating": np.asarray(L0_attn_gating),
        "base_wT": np.asarray(L0_ffn_base_w).T,
        "base_b": np.asarray(L0_ffn_base_b),
        "arT": np.concatenate([np.asarray(L0_ffn_A), np.asarray(L0_ffn_router_w)]).T,
        "B_T": np.asarray(L0_ffn_B).transpose(0, 2, 1).reshape(E * R, C),
    }
    arrays.update(constants())
    arrays = {k: np.ascontiguousarray(v) for k, v in arrays.items()}
    nc = bacc.Bacc("TRN2", target_bir_lowering=False, num_devices=1)
    d = {k: nc.dram_tensor("in_" + k, v.shape, mybir.dt.from_np(v.dtype), kind="ExternalInput").ap() for k, v in arrays.items()}
    d["out"] = nc.dram_tensor("out", (NB * T, C), F32, kind="ExternalOutput").ap()
    build(nc, d)
    r = run_bass_kernel_spmd(nc, [{"in_" + k: v for k, v in arrays.items()}], core_ids=[0])
    return r.results[0]["out"].reshape(NB, T, C)
```

```python
from contextlib import ExitStack

import concourse.bass as bass
from concourse import mybir

F32 = mybir.dt.float32
F32R = mybir.dt.float32r
I32 = mybir.dt.int32
BF16 = mybir.dt.bfloat16
ALU = mybir.AluOpType
ACT = mybir.ActivationFunctionType
AX = mybir.AxisListType

NB, T, C, H = 2, 1024, 512, 32
HD = C // H
J = 10
E, R = 16, 64
P = 128
CC = C // P
TT = 512
NTT = T // TT
BANK = 512
HG = 4
GB = H // HG
G = NB * GB
QT = T // P
PARTS = 3
TERMS = [(0, 0), (0, 1), (0, 2), (1, 0), (1, 1), (2, 0)]
KR = len(TERMS) * HD
KX = KR + 2
NEG = -3.0e38
VW = 32
EPS = 1e-5
NEWTON = 3
NORM_STEPS = 4 + 3 * NEWTON


HEAD_START = {"yadd": ("gp", 2), "uf": ("pe", 4), "tm": ("ve", 8), "ro": ("ve", 2), "rem": ("gp", 2),
              "p3": ("gp", 2), "vr": ("act", 2), "asub": ("ve", 2), "xh": ("act", 2), "xl": ("ve", 2), "pst0": ("sp", 16), "pst1": ("sp", 16)}


MAX_BANKS = [
    [(0, 0, 1), (2, 0, 3)],
    [(1, 0, 2), (5, 4, 2)],
    [(3, 0, 4)],
    [(4, 0, 4)],
    [(4, 4, 1), (6, 4, 3)],
    [(5, 0, 4)],
    [(6, 0, 4)],
    [(7, 0, 4)],
    [(7, 4, 4)],
]
NMB = len(MAX_BANKS)
NMX = HG * NMB
LEAD = NMB
NORM = [(0, 4), (4, 4)]
ROWS_LAG = 3
LAG = 2
NORM_STEP = 4
ORDER = [0, 7, 1, 6, 2, 5, 3, 4]
CHUNKS = [-(-(T - kb * P) // BANK) for kb in ORDER]
SCORE_BANKS = HG * sum(CHUNKS)
SCORE_BUFS, MAX_BUFS = 3, 3
assert SCORE_BANKS % SCORE_BUFS == 0
assert LAG == 2
LAST_TILE = [max((k for k in range(BANK // P * (n + 1))), key=ORDER.index) for n in range(T // BANK)]
assert ORDER[0] == 0
NORM_COLUMNS = 1200
BANK_EVERY = (HG * P * QT * (QT + 1) - len(NORM) * NORM_COLUMNS) // NMX
NTC = NB * QT
CW = [("w_projT", 0), ("base_wT", 0), ("B_T", 0), ("B_T", CC)]


def runs(pick):
    out, r = [], 0
    while r < len(TERMS):
        n = 1
        while r + n < len(TERMS) and TERMS[r + n][pick] == TERMS[r + n - 1][pick] + 1:
            n += 1
        out.append((r, n, TERMS[r][pick]))
        r += n
    return out


GROUP_LOADS = len(runs(0)) + len(runs(1))


class Group:

    def __init__(self, g, m, v):
        self.g, self.m, self.v, self.fixed = g, m, v, isinstance(g, int)

    def plus(self, n):
        return Group(self.g + n, (self.m + n) % 3, self.v + (self.m + n) // 3)

    def has(self, n):
        return not self.fixed or 0 <= self.g + n < G


def value_pieces(kb):
    return [(max(q0, kb * P), q0 + BANK) for q0 in range(0, T, BANK) if kb * P < q0 + BANK]


def items(gr):
    todo = ([(1, w) for w in range(LEAD, NMX)] if gr.has(1) else []) + ([(2, w) for w in range(LEAD)] if gr.has(2) else [])
    out, off, rows_in = [], 0, None

    def bank_items(n):
        nonlocal off, rows_in
        for _ in range(n):
            if rows_in == 0 or (rows_in is not None and not todo):
                out.append(("rows", 1, off))
                off += 1
                rows_in = None
            if not todo:
                return
            n_, w = todo.pop(0)
            out.append(("max", n_, w, off))
            off += 1
            if rows_in is not None:
                rows_in -= 1
            if (n_, w) == (1, NMX - 1):
                out.append(("calc", 1, off))
                rows_in = ROWS_LAG

    due = 0
    for st in range(QT):
        back = -1 if st < LAG else 0
        kv = ORDER[(st - LAG) % QT]
        values = [("pv", back, kv) + v for v in value_pieces(kv)] if gr.has(back) else []
        chunks = HG * CHUNKS[st]
        for c in range(chunks):
            h, c0 = divmod(c, CHUNKS[st])
            work = [(("score", st, h, c0), min(BANK, T - ORDER[st] * P - c0 * BANK))]
            for n, v in enumerate(values):
                if c + 1 == -(-chunks * (n + 1) // (len(values) + 1)):
                    work.append((v, HG * (v[4] - v[3])))
            for it, time in work:
                if 2 * due + time >= 2 * BANK_EVERY:
                    bank_items(1)
                    due -= BANK_EVERY
                out.append(it)
                due += time
                while due >= BANK_EVERY:
                    bank_items(1)
                    due -= BANK_EVERY
            if c0 > 0:
                continue
            if st == NORM_STEP and h < len(NORM) and gr.has(-1):
                out.append(("norm", h, off))
                off += 1
                due -= NORM_COLUMNS
    bank_items(NMX)
    if rows_in is not None:
        bank_items(1)
    return out, off


PRO = NMX + 1 + (LEAD if G > 1 else 0)
USE0 = [PRO]
for _g in range(G):
    USE0.append(USE0[-1] + items(Group(_g, _g % 3, _g // 3))[1])
STEADY = USE0[2] - USE0[1]
assert STEADY % MAX_BUFS == 0 and all(USE0[n + 1] - USE0[n] == STEADY for n in range(1, G - 2))
PSM_TOTAL = USE0[G] + len(NORM)


def use_of(gr, off):
    if gr.fixed:
        return USE0[gr.g] + off, (USE0[gr.g] + off) % MAX_BUFS
    return gr.g * STEADY + (USE0[1] - STEADY + off), (USE0[1] + off) % MAX_BUFS


def score_chunks(gr, st, h):
    width = T - ORDER[st] * P
    for c in range(CHUNKS[st]):
        off = HG * sum(CHUNKS[:st]) + h * CHUNKS[st] + c
        yield gr.g * SCORE_BANKS + off, off % SCORE_BUFS, c * BANK, min(BANK, width - c * BANK)


def norm_end(gr):
    offs = [x[2] for x in items(gr)[0] if x[0] == "norm"]
    return use_of(gr, offs[-1] + 1)[0]


def drive(eng, group):
    group(Group(0, 0, 0))
    with eng.Fori(0, 4) as i:
        for k in range(1, 4):
            group(Group(3 * i + k, k % 3, i + k // 3))
    for g in range(13, G):
        group(Group(g, g % 3, g // 3))


def drive_tiles(eng, step):
    for j in range(4):
        step(j, j % 2)
    with eng.Fori(0, NTC // 2 - 3) as i:
        for k in range(2):
            step(2 * i + (4 + k), k)
    for j in range(NTC - 2, NTC + 2):
        step(j, j % 2)


def build(nc, d):
    with ExitStack() as ctx:
        def sem(name):
            return ctx.enter_context(nc.semaphore(name))

        def psum(name, cols, dt=F32):
            return ctx.enter_context(nc.psum_tensor(name, [P, cols], dt))

        def sb(stack, name, shape, dt=F32):
            return stack.enter_context(nc.sbuf_tensor(name, shape, dt))

        q_parts = nc.dram_tensor("q_parts", (NB * H, PARTS, HD, T), BF16, kind="Internal").ap()
        k_parts = nc.dram_tensor("k_parts", (NB * H, PARTS, HD, T), BF16, kind="Internal").ap()

        ident = sb(ctx, "ident", [P, P])
        identb = sb(ctx, "identb", [P, P], BF16)
        cmask = sb(ctx, "cmask", [P, P])
        v_all = sb(ctx, "v_all", [P, G, QT, HG * HD])
        y_all = sb(ctx, "y_all", [P, G, QT, HG * HD])

        with ExitStack() as a:
            cs = sb(a, "cs", [P, 2, T])
            rope = [sb(a, f"rope{i}", [P, 2, TT]) for i in range(2)]
            rem = sb(a, "rem", [P, 2, TT])
            xh, xl = [None, None], [None, None]
            for i in range(2):
                xh[i] = sb(a, f"xh{i}", [P, CC, TT], F32R)
                xl[i] = sb(a, f"xl{i}", [P, CC, TT], F32R)
            wh = sb(a, "wh", [P, CC, 3 * C], F32R)
            wl = sb(a, "wl", [P, CC, 3 * C], F32R)
            xs = sb(a, "xs", [P, 2, TT])
            rtmp = [sb(a, f"rtmp{i}", [P, TT]) for i in range(2)]
            part = [sb(a, f"part{i}", [P, PARTS, 2, TT], BF16) for i in range(2)]
            pat = [sb(a, f"pat{i}", [80, 4, P]) for i in range(2)]
            gate = sb(a, "gate", [P, 1])
            akm = sb(a, "akm", [P, 16])
            avm = sb(a, "avm", [80, 8])
            akbd = sb(a, "akbd", [P, 2, 2, 16, J])
            avbd = sb(a, "avbd", [80, 4, P])
            asum = sb(a, "asum", [P, 4, H])
            with ExitStack() as a0:
                at_raw = sb(a0, "at_raw", [P, CC, J])
                ath = sb(a0, "ath", [P, CC, 80], F32R)
                atl = sb(a0, "atl", [P, CC, 80], F32R)
            with ExitStack() as a1:
                asb = [sb(a1, f"asb{i}", [P, H, J]) for i in range(2)]
                pa = [sb(a1, f"pa{i}", [P, H, J]) for i in range(4)]
        bc = ctx.enter_context(ExitStack())
        wph = sb(bc, "wph", [P, CC, C], F32R)
        wpl = sb(bc, "wpl", [P, CC, C], F32R)
        ar_w = sb(bc, "ar_w", [P, CC, R + E])
        rev = sb(bc, "rev", [P, E])
        sb(bc, "spare", [P, 688])
        with ExitStack() as b:
            qs, ks = [None] * 3, [None] * 3
            for i in range(3):
                qs[i] = sb(b, f"qs{i}", [P, HG, T], BF16)
                ks[i] = sb(b, f"ks{i}", [P, HG, T], BF16)
            vb = [sb(b, f"vb{i}", [P, QT, HG, VW]) for i in range(3)]
            mx = [sb(b, f"mx{i}", [P, 3, HG, QT]) for i in range(3)]
            mall = sb(b, "mall", [P, HG * QT])
            mneg = sb(b, "mneg", [P, 2, HG * QT], BF16)
            mrow = [sb(b, f"mrow{i}", [2 * HG * QT, P], BF16) for i in range(3)]
            yts = sb(b, "yts", [P, T])
            rden = sb(b, "rden", [P, QT, HG])
            ynew = sb(b, "ynew", [P, QT, HG, HD])
            pt = [sb(b, f"pt{i}", [P, HG, T]) for i in range(3)]
        with ExitStack() as c:
            wfh = sb(c, "wfh", [P, CC, C], F32R)
            wfl = sb(c, "wfl", [P, CC, C], F32R)
            wbh = sb(c, "wbh", [P, 8, C], F32R)
            wbl = sb(c, "wbl", [P, 8, C], F32R)
            xin = [sb(c, f"xin{i}", [P, C]) for i in range(2)]
            ytile = [sb(c, f"ytile{i}", [P, C]) for i in range(2)]
            yth = [sb(c, f"yth{i}", [P, CC, P], F32R) for i in range(2)]
            ytl = [sb(c, f"ytl{i}", [P, CC, P], F32R) for i in range(2)]
            xth = [sb(c, f"xth{i}", [P, CC, P], F32R) for i in range(2)]
            xtl = [sb(c, f"xtl{i}", [P, CC, P], F32R) for i in range(2)]
            x1 = [sb(c, f"x1_{i}", [P, C]) for i in range(2)]
            xb = [sb(c, f"xb{i}", [P, C]) for i in range(2)]
            bias = sb(c, "bias", [P, C])
            gbuf = [sb(c, f"g{i}", [P, E, R]) for i in range(2)]
            gth = sb(c, "gth", [P, 8, P], F32R)
            gtl = sb(c, "gtl", [P, 8, P], F32R)
            outb = [sb(c, f"outb{i}", [P, C]) for i in range(2)]
            hr = [sb(c, f"hr{i}", [P, R]) for i in range(2)]
            ex = [sb(c, f"ex{i}", [P, E]) for i in range(2)]
            sm = sb(c, "sm", [P, 72])
            rt = sb(c, "rt", [P, 8, E])
            comb = [sb(c, f"comb{i}", [P, E]) for i in range(2)]

        bank = [psum(f"bank{i}", 2 * 512) for i in range(4)]

        def half(i, dt=None):
            return bank[i // 2][:, 512 * (i % 2):512 * (i % 2) + 512]

        def max_out(i):
            return half(SCORE_BUFS + i)

        block = ctx.enter_context(nc.Block())
        s = {}

        def at(eng, name, value, apart=False):
            if isinstance(value, int) and value <= 0:
                return
            value = value + HEAD_START.get(name, (None, 0))[1]
            eng.wait_ge(S(name), value)
            if apart and not isinstance(value, int):
                eng.sem_inc(S("carrier"), 1)

        def give_head_start(eng, who):
            for name, (by, n) in HEAD_START.items():
                if by == who:
                    eng.nop().then_inc(S(name), n)

        def S(name):
            if name not in s:
                s[name] = sem(name)
            return s[name]

        def three(pe, out, lh, ll, rh, rl, first, last):
            pe.matmul(out, lh, rh, start=first, stop=False)
            pe.matmul(out, ll, rh, start=False, stop=False)
            return pe.matmul(out, lh, rl, start=False, stop=last)

        NU = 4
        NV = 12
        TILES = NB * NTT
        xT_d = d["xT"].rearrange("(c p) t -> p c t", p=P)
        wT_d = d["w_attnT"].rearrange("(c p) n -> p c n", p=P)
        y_flat = y_all[:].rearrange("p g q n -> p (g q n)")
        v_flat = v_all[:].rearrange("p g q n -> p (g q n)")
        wst = [v_flat[:, i * CC * C:(i + 1) * CC * C].rearrange("p (c n) -> p c n", c=CC) for i in range(4)]

        def cw_dst(n):
            return [(wph[:], wpl[:]), (wfh[:], wfl[:]),
                    (wbh[:, 0:CC], wbl[:, 0:CC]), (wbh[:, CC:], wbl[:, CC:])][n]

        def split_high(act, n):
            at(act, f"cw{n}_ld", 16)
            act.copy(cw_dst(n)[0], wst[n]).then_inc(S("cwh"), 1)

        def split_low(ve, n):
            at(ve, "cwh", n + 1)
            ve.tensor_tensor(cw_dst(n)[1], wst[n], cw_dst(n)[0], ALU.subtract).then_inc(S("cwl"), 1)

        w_raw = y_flat[:, 0:CC * 3 * C].rearrange("p (c n) -> p c n", c=CC)

        @block.sync
        def _(sp):
            give_head_start(sp, "sp")
            for i in range(3):
                sp.dma_start(w_raw[:, :, i * C:(i + 1) * C], wT_d[:, :, i * C:(i + 1) * C]).then_inc(S(f"w{i}_ld"), 16)
                if i == 0:
                    sp.dma_start(at_raw[:], d["adapterT"].rearrange("(c p) j -> p c j", p=P)).then_inc(S("c_ld"), 16)
                    sp.dma_start(cs[:], d["cos_sin"]).then_inc(S("c_ld"), 16)
                    sp.dma_start(ident[:], d["ident"]).then_inc(S("c_ld"), 16)
                    sp.dma_start(akm[:], d["akm"]).then_inc(S("c_ld"), 16)
                    sp.dma_start(avm[:], d["avm"]).then_inc(S("c_ld"), 16)
                    sp.dma_start(cmask[:], d["cmask"]).then_inc(S("c_ld"), 16)
                    sp.dma_start(gate[:], d["gating"].partition_broadcast(P)).then_inc(S("c_ld"), 16)

            def load_x(b, u, tau, hf):
                at(sp, "xh", 2 * tau + hf)
                at(sp, "xl", 2 * tau + hf)
                sp.dma_start(xs[:], xT_d[:, 2 * hf:2 * hf + 2, b * T + u * TT:b * T + (u + 1) * TT]).then_inc(S("x_ld"), 16)

            def store_unit(b, u, tau, j):
                n = 4 * tau + j
                dst = (q_parts if j < 2 else k_parts)[bass.ds(b * H + (j % 2) * 16, 16)]
                at(sp, "p3", n + 1)
                for r in range(PARTS):
                    for hf in range(2):
                        sp.dma_start(dst[:, r, 8 * hf:8 * hf + 8, u * TT:(u + 1) * TT],
                                     part[j % 2][:, r, hf, :]).then_inc(S(f"pst{j % 2}"), 16)

            def load_group(gr):
                if not (gr.fixed and gr.g < 3):
                    at(sp, "sc", SCORE_BANKS * (gr.g - 2))
                for dst, src, pick in ((qs[gr.m], q_parts, 0), (ks[gr.m], k_parts, 1)):
                    for r, n, p0 in runs(pick):
                        sp.dma_start(dst[HD * r:HD * (r + n), :, :],
                                     src[bass.ds(gr.g * HG, HG), p0:p0 + n].rearrange("h s d t -> (s d) h t")
                                     ).then_inc(S(f"grp{gr.m}"), 16)

            def load_first():
                at(sp, "xh", 2 * TILES + 2)
                at(sp, "xl", 2 * TILES + 2)
                for n in range(2):
                    at(sp, f"pst{n}", 16 * 6 * NTT * 2)
                load_group(Group(0, 0, 0))

            for hf in range(2):
                load_x(0, 0, 0, hf)
            for b in range(NB):
                for u in range(NTT):
                    tau = NTT * b + u
                    following = divmod((tau + 1) % TILES, NTT)
                    load_x(*following, tau + 1, 0)
                    store_unit(b, u, tau, 0)
                    store_unit(b, u, tau, 1)
                    load_x(*following, tau + 1, 1)
                    store_unit(b, u, tau, 2)
                    if tau == TILES - 1:
                        load_first()
                    store_unit(b, u, tau, 3)

            def store_max(gr, use):
                at(sp, "mr", use + 1)
                sp.dma_start(qs[gr.m][KR:KX].rearrange("s h (q t) -> s (h q) t", t=P), mrow[gr.m][:]
                             ).then_inc(S(f"mrow{gr.m}"), 16)

            at(sp, "vf", NV * TILES)
            load_group(Group(1, 1, 0))
            for n in range(2):
                at(sp, f"pst{n}", 16 * 6 * TILES * 2)
            sp.nop().then_inc(S("boundary_b"), 1)

            def load_weight(n):
                name, k0 = CW[n]
                sp.dma_start(wst[n], d[name].rearrange("(c p) n -> p c n", p=P)[:, k0:k0 + CC]).then_inc(S(f"cw{n}_ld"), 16)

            def sp_group(gr):
                if gr.has(2):
                    load_group(gr.plus(2))
                if gr.fixed and gr.g == G - 2:
                    at(sp, "vb", GB)
                    for n in range(2):
                        load_weight(n)
                    sp.dma_start(ar_w[:], d["arT"].rearrange("(c p) n -> p c n", p=P)).then_inc(S("ar_ld"), 16)
                    sp.dma_start(rev[:], d["rev"]).then_inc(S("cc_ld"), 16)
                if gr.fixed and gr.g == G - 1:
                    at(sp, "vb", G)
                    for n in (2, 3):
                        load_weight(n)
                for it in items(gr)[0]:
                    if it[0] == "rows":
                        store_max(gr.plus(1), use_of(gr, it[2])[0])

            store_max(Group(0, 0, 0), NMX)
            drive(sp, sp_group)

            at(sp, "boundary_c", 4)
            sp.dma_start(bias[:], d["base_b"].partition_broadcast(P)).then_inc(S("cc_ld"), 16)
            x_d, o_d = d["x"], d["out"]

            def load_xin(t, m):
                at(sp, "x1", t - 1)
                sp.dma_start(xin[m][:], x_d[bass.ds(t * P, P), :]).then_inc(S(f"xin{m}"), 16)

            def store_out(t, m):
                at(sp, "fin", t + 1)
                sp.dma_start(o_d[bass.ds(t * P, P), :], outb[m][:]).then_inc(S(f"ost{m}"), 16)

            load_xin(0, 0)

            def sp_c(j, m):
                if not isinstance(j, int) or j + 1 < NTC:
                    load_xin(j + 1, 1 - m)
                if not isinstance(j, int) or j >= 2:
                    store_out(j - 2, m)

            drive_tiles(sp, sp_c)
            for m in range(2):
                at(sp, f"ost{m}", 16 * NTC // 2)

        @block.gpsimd
        def _(gp):
            give_head_start(gp, "gp")
            def remainders(tau, j):
                n = 4 * tau + j
                at(gp, "p1", n + 1)
                at(gp, "p3", n)
                gp.tensor_tensor(rem[:], rope[j % 2][:], part[j % 2][:, 0], ALU.subtract).then_inc(S("rem"), 1)
                at(gp, "p2", n + 1)
                at(gp, "rem", n + 1)
                gp.tensor_tensor(part[j % 2][:, 2], rem[:], part[j % 2][:, 1], ALU.subtract).then_inc(S("p3"), 1)

            with gp.Fori(0, NB) as b:
                for u in range(NTT):
                    for j in range(NU):
                        remainders(NTT * b + u, j)
            at(gp, "p3", 4 * TILES)
            gp.nop().then_inc(S("boundary_b"), 1)
            at(gp, "boundary_b", 5)
            for i in range(3):
                gp.memset(vb[i][:, :, :, HD:HD + 1], 1.0).then_inc(S("vset"), 1)
                gp.memset(vb[i][:, :, :, HD + 1:VW], 0.0).then_inc(S("vset"), 1)
            for i in range(3):
                at(gp, "vset", 6 + i)
                gp.memset(ks[i][KR:KX], 1.0).then_inc(S("vset"), 1)

            def add_heads(gr, i, use):
                q0, nq = NORM[i]
                at(gp, "mr", use + 1)
                ydst = y_all[:, bass.ds(gr.g, 1), q0:q0 + nq].rearrange("p a q n -> p (a q n)")
                gp.tensor_tensor(ydst, ydst, ynew[:, q0:q0 + nq].rearrange("p q h e -> p (q h e)"),
                                 ALU.add).then_inc(S("yadd"), 1)

            def gp_group(gr):
                for st, kb in enumerate(ORDER):
                    i = st - NORM_STEP - 1
                    if 0 <= i < len(NORM) and gr.has(-1):
                        off, = [x[2] for x in items(gr)[0] if x[:2] == ("norm", i)]
                        add_heads(gr.plus(-1), i, use_of(gr, off)[0])
                    at(gp, "ex", gr.g * SCORE_BANKS + HG * sum(CHUNKS[:st + 1]), apart=True)
                    blk = pt[(QT * gr.m + st) % 3][:, :, kb * P:(kb + 1) * P]
                    gp.affine_select(out=blk, in_=blk, compare_op=ALU.is_ge, fill=0.0, base=0,
                                     pattern=[[0, HG], [1, P]], channel_multiplier=-1).then_inc(S("dg"), 1)

            drive(gp, gp_group)
            for i in range(len(NORM)):
                add_heads(Group(G - 1, (G - 1) % 3, (G - 1) // 3), i, USE0[G] + i)
            at(gp, "dg", 8 * G)
            at(gp, "yadd", len(NORM) * G)
            gp.nop().then_inc(S("boundary_c"), 1)
            at(gp, "boundary_c", 4)
            at(gp, "cc_ld", 32)

            def add_bias(t, m):
                at(gp, "x1", t + 1)
                at(gp, "fin", t - 1)
                gp.tensor_tensor(xb[m][:], x1[m][:], bias[:], ALU.add).then_inc(S("xb"), 1)

            def expand(t, m):
                at(gp, "comb", t + 1)
                at(gp, "hr", t + 1)
                at(gp, "tg", t - 1)
                gp.tensor_tensor(gbuf[m][:], comb[m][:].unsqueeze(2).to_broadcast([P, E, R]),
                                 hr[m][:].unsqueeze(1).to_broadcast([P, E, R]), ALU.mult).then_inc(S("g"), 1)

            def gp_c(j, m):
                if not isinstance(j, int) or 1 <= j <= NTC:
                    expand(j - 1, 1 - m)
                    add_bias(j - 1, 1 - m)

            drive_tiles(gp, gp_c)

        @block.scalar
        def _(act):
            give_head_start(act, "act")
            for i in range(3):
                at(act, f"w{i}_ld", 16)
                act.copy(wh[:, :, i * C:(i + 1) * C], w_raw[:, :, i * C:(i + 1) * C]).then_inc(S("wh"), 1)
                if i == 0:
                    at(act, "c_ld", 16 * 7)
                    act.copy(ath[:].rearrange("p c (h j) -> p c h j", j=J),
                             at_raw[:].unsqueeze(2).to_broadcast([P, CC, 8, J])).then_inc(S("ath"), 1)

            def x_high(tau, m, hf):
                at(act, "x_ld", 16 * (2 * tau + hf + 1))
                at(act, "uf", NU * (tau - 1))
                act.copy(xh[m][:, 2 * hf:2 * hf + 2], xs[:]).then_inc(S("xh"), 1)

            def first(tau, j):
                n = 4 * tau + j
                at(act, "ro", n + 1)
                at(act, f"pst{j % 2}", 16 * 6 * (2 * tau + j // 2))
                act.copy(part[j % 2][:, 0], rope[j % 2][:]).then_inc(S("p1"), 1)

            def second(tau, j):
                at(act, "rem", 4 * tau + j + 1)
                act.copy(part[j % 2][:, 1], rem[:]).then_inc(S("p2"), 1)

            def evac(tau, w, out, src):
                at(act, "vf", NV * tau + w + 1)
                act.copy(out, src).then_inc(S("vr"), 1)

            def exp_a(tau, a_):
                m = 4 * tau + a_
                at(act, "asub", m + 1)
                act.activation(asb[a_ % 2][:], asb[a_ % 2][:], ACT.Exp, scale=float(C) ** -0.5).then_inc(S("aex"), 1)

            for hf in range(2):
                x_high(0, 0, hf)

            with act.Fori(0, NB) as b:
                for u in range(NTT):
                    tau = NTT * b + u

                    def v_out(a_):
                        return v_all[:, bass.ds(b * GB, GB), u * 4 + a_, :]

                    def y_out(a_):
                        return y_all[:, bass.ds(b * GB, GB), u * 4 + a_, :]

                    def vb_(w):
                        return half(4 + w % 2)

                    first(tau, 0)
                    evac(tau, 0, v_out(0), vb_(0).rearrange("p (g n) -> p g n", g=GB))
                    second(tau, 0)
                    evac(tau, 1, v_out(1), vb_(1).rearrange("p (g n) -> p g n", g=GB))
                    first(tau, 1)
                    evac(tau, 2, v_out(2), vb_(2).rearrange("p (g n) -> p g n", g=GB))
                    evac(tau, 3, v_out(3), vb_(3).rearrange("p (g n) -> p g n", g=GB))
                    second(tau, 1)
                    for a_ in range(4):
                        exp_a(tau, a_)
                    x_high(tau + 1, 1 - u, 0)
                    evac(tau, 4, pat[0][:], vb_(4)[0:80].rearrange("p (g n) -> p g n", g=4))
                    evac(tau, 5, pat[1][:], vb_(5)[0:80].rearrange("p (g n) -> p g n", g=4))
                    evac(tau, 6, y_out(0), vb_(6).rearrange("p (g n) -> p g n", g=GB))
                    evac(tau, 7, y_out(1), vb_(7).rearrange("p (g n) -> p g n", g=GB))
                    first(tau, 2)
                    x_high(tau + 1, 1 - u, 1)
                    evac(tau, 8, pat[0][:], vb_(8)[0:80].rearrange("p (g n) -> p g n", g=4))
                    evac(tau, 9, pat[1][:], vb_(9)[0:80].rearrange("p (g n) -> p g n", g=4))
                    second(tau, 2)
                    first(tau, 3)
                    evac(tau, 10, y_out(2), vb_(10).rearrange("p (g n) -> p g n", g=GB))
                    evac(tau, 11, y_out(3), vb_(11).rearrange("p (g n) -> p g n", g=GB))
                    second(tau, 3)
            at(act, "p2", 4 * TILES)
            act.nop().then_inc(S("boundary_b"), 1)
            at(act, "boundary_b", 5)

            def build_v(gr):
                if not (gr.fixed and gr.g < 3):
                    at(act, "pv", QT * (gr.g - 2))
                act.copy(vb[gr.m][:, :, :, 0:HD],
                         v_all[:, bass.ds(gr.g, 1)].rearrange("p a q (h e) -> p (a q) h e", e=HD)).then_inc(S("vb"), 1)

            def evac_y(gr, i):
                at(act, "pv", QT * (gr.g + 1) - 1 + i)
                if gr.has(-1):
                    at(act, "mf", norm_end(gr))
                act.copy(yts[:, i * BANK:(i + 1) * BANK], bank[3][:, i * BANK:(i + 1) * BANK]).then_inc(S("yts"), 1)

            def act_group(gr):
                for st, kb in enumerate(ORDER):
                    n = QT * gr.g + st
                    if not (gr.fixed and n < 3):
                        at(act, "pv", n - 2)
                    for h in range(HG):
                        for n, bk, c0, w in score_chunks(gr, st, h):
                            at(act, "sc", n + 1)
                            act.activation(pt[(QT * gr.m + st) % 3][:, h, kb * P + c0:kb * P + c0 + w], half(bk)[:, 0:w],
                                           ACT.Exp, scale=float(HD) ** -0.5).then_inc(S("ex"), 1)
                        if st < LAG and h == HG - 1 and gr.has(-1):
                            evac_y(gr.plus(-1), st)
                    if st == 3 and gr.has(1):
                        build_v(gr.plus(1))
                    if st == 3 and not gr.has(1):
                        split_high(act, 0)

            build_v(Group(0, 0, 0))
            drive(act, act_group)
            for i in range(2):
                evac_y(Group(G - 1, (G - 1) % 3, (G - 1) // 3), i)
            at(act, "yts", 2 * G)
            act.nop().then_inc(S("boundary_c"), 1)
            at(act, "boundary_c", 4)

            def tile_y(t, m):
                at(act, "ty", t - 1)
                bb, qt = t >> 3, t & 7
                if not isinstance(t, int):
                    bb = nc.s_assert_within(bb, 0, NB - 1, skip_runtime_bounds_check_because="t < NB * QT")
                act.copy(ytile[m][:].rearrange("p (g n) -> p g n", g=GB),
                         y_all[:, bass.ds(bb * GB, GB), bass.ds(qt, 1), :].rearrange("p g a n -> p g (a n)")
                         ).then_inc(S("yt"), 1)

            def hi_x(t, m):
                at(act, "tx", t + 1)
                act.copy(xth[m][:].rearrange("p c n -> p (c n)"), half(0)).then_inc(S("xth"), 1)

            def hi_g(t):
                at(act, "tg", t + 1)
                act.copy(gth[:].rearrange("p c n -> p (c n)"), bank[3][:]).then_inc(S("gth"), 1)

            def router_exp(t, m):
                at(act, "nmax", t + 1)
                act.copy(hr[m][:], half(3)[:, 0:R]).then_inc(S("hr"), 1)
                act.activation(ex[m][:], half(3)[:, R:R + E], ACT.Exp, bias=sm[:, 8 + 2 * m:9 + 2 * m], scale=1.0,
                               accum_out=sm[:, 9 + 2 * m:10 + 2 * m]).then_inc(S("rex"), 1)

            def hi_y(t, m):
                at(act, "ty", t + 1)
                act.copy(yth[m][:].rearrange("p c n -> p (c n)"), half(1)).then_inc(S("yth"), 1)

            tile_y(0, 0)
            hi_y(0, 0)
            split_high(act, 1)
            tile_y(1, 1)

            def act_c(j, m):
                sure = not isinstance(j, int)
                if not sure and j == 1:
                    split_high(act, 2)
                    split_high(act, 3)
                if sure or 1 <= j <= NTC:
                    hi_x(j - 1, 1 - m)
                if sure or 2 <= j:
                    hi_g(j - 2)
                if sure or j + 1 < NTC:
                    hi_y(j + 1, 1 - m)
                if sure or 1 <= j <= NTC:
                    router_exp(j - 1, 1 - m)
                if sure or j + 2 < NTC:
                    tile_y(j + 2, m)

            drive_tiles(act, act_c)

        @block.vector
        def _(ve):
            give_head_start(ve, "ve")
            for i in range(3):
                at(ve, "wh", i + 1)
                ve.tensor_tensor(wl[:, :, i * C:(i + 1) * C], w_raw[:, :, i * C:(i + 1) * C],
                                 wh[:, :, i * C:(i + 1) * C], ALU.subtract).then_inc(S("wl"), 1)
                if i == 0:
                    at(ve, "ath", 1)
                    ve.tensor_tensor(atl[:].rearrange("p c (h j) -> p c h j", j=J),
                                     at_raw[:].unsqueeze(2).to_broadcast([P, CC, 8, J]),
                                     ath[:].rearrange("p c (h j) -> p c h j", j=J), ALU.subtract).then_inc(S("atl"), 1)
                    ve.tensor_copy(identb[:], ident[:]).then_inc(S("idb"), 1)

            def x_low(tau, m, hf):
                at(ve, "xh", 2 * tau + hf + 1)
                ve.tensor_tensor(xl[m][:, 2 * hf:2 * hf + 2], xs[:], xh[m][:, 2 * hf:2 * hf + 2],
                                 ALU.subtract).then_inc(S("xl"), 1)

            x_low(0, 0, 0)
            at(ve, "akf", 1)
            ak_sb = rope[0][0:80, 0, :]
            ve.tensor_copy(ak_sb, half(6)[0:80]).then_inc(S("aks"), 1)
            at(ve, "avf", 1)
            ve.tensor_tensor(avbd[:].rearrange("p a (h e) -> p a h e", e=HD),
                             half(7)[0:80].rearrange("p (a h e) -> p a h e", a=4, e=HD),
                             avm[:].unsqueeze(1).unsqueeze(3).to_broadcast([80, 4, 8, HD]), ALU.mult).then_inc(S("avbd"), 1)
            at(ve, "akt", 1)
            for hg in range(2):
                for hf in range(2):
                    i = 2 * hg + hf
                    ve.tensor_tensor(akbd[:, hg, hf],
                                     akm[:].unsqueeze(2).to_broadcast([P, 16, J]),
                                     half(6)[:, 80 * i:80 * i + J].unsqueeze(1).to_broadcast([P, 16, J]),
                                     ALU.mult).then_inc(S("akbd"), 1)

            x_low(0, 0, 1)

            def rotate(tau, u, j):
                n = 4 * tau + j
                at(ve, "uf", n + 1)
                a_, b_ = half(2 * (j % 2)), half(2 * (j % 2) + 1)
                cos, sin = (cs[:, i, u * TT:(u + 1) * TT] for i in range(2))
                ro = rope[j % 2]
                at(ve, "rem", n - 1)
                if j >= 2:
                    at(ve, "as", 4 * tau + 4)
                at(ve, "ro", n)
                ve.tensor_tensor(ro[:, 0], a_, cos, ALU.mult).then_inc(S("tm"), 1)
                ve.tensor_tensor(rtmp[0][:], b_, sin, ALU.mult).then_inc(S("tm"), 1)
                ve.tensor_tensor(ro[:, 1], b_, cos, ALU.mult).then_inc(S("tm"), 1)
                ve.tensor_tensor(rtmp[1][:], a_, sin, ALU.mult).then_inc(S("tm"), 1)
                at(ve, "tm", 4 * (n + 1))
                ve.tensor_tensor(ro[:, 0], ro[:, 0], rtmp[0][:], ALU.subtract)
                ve.tensor_tensor(ro[:, 1], ro[:, 1], rtmp[1][:], ALU.add).then_inc(S("ro"), 1)

            def soft_a(tau, a_):
                m = 4 * tau + a_
                at(ve, "as", m + 1)
                sc = half(6 + a_ % 2)[:, 0:H * J].rearrange("p (h j) -> p h j", j=J)
                ve.tensor_reduce(asum[:, 0], sc, AX.X, ALU.max).then_inc(S("ad"), 1)
                at(ve, "ad", 5 * m + 1)
                ve.tensor_tensor(asb[a_ % 2][:], sc, asum[:, 0].unsqueeze(2).to_broadcast([P, H, J]),
                                 ALU.subtract).then_inc(S("asub"), 1)
                at(ve, "aex", m + 1)
                ve.tensor_reduce(asum[:, 1], asb[a_ % 2][:], AX.X, ALU.add).then_inc(S("ad"), 1)
                at(ve, "ad", 5 * m + 2)
                ve.reciprocal(asum[:, 2], asum[:, 1]).then_inc(S("ad"), 1)
                at(ve, "ad", 5 * m + 3)
                ve.tensor_scalar(asum[:, 3], asum[:, 2], gate[:, 0:1], None, ALU.mult).then_inc(S("ad"), 1)
                at(ve, "ad", 5 * m + 4)
                ve.tensor_tensor(pa[a_][:], asb[a_ % 2][:], asum[:, 3].unsqueeze(2).to_broadcast([P, H, J]),
                                 ALU.mult).then_inc(S("ad"), 1)

            with ve.Fori(0, NB) as b:
                for u in range(NTT):
                    tau = NTT * b + u
                    rotate(tau, u, 0)
                    rotate(tau, u, 1)
                    for a_ in range(4):
                        soft_a(tau, a_)
                    x_low(tau + 1, 1 - u, 0)
                    rotate(tau, u, 2)
                    x_low(tau + 1, 1 - u, 1)
                    rotate(tau, u, 3)
            at(ve, "ro", 4 * TILES)
            at(ve, "xl", 2 * TILES + 2)
            ve.nop().then_inc(S("boundary_b"), 1)
            at(ve, "vf", NV * TILES)

            for m in range(3):
                ve.memset(mx[m][:], NEG).then_inc(S("mset"), 1)
            at(ve, "mset", 3)

            def max_bank(gr, w, use, bk):
                h, pieces = w // NMB, MAX_BANKS[w % NMB]
                at(ve, "mf", use + 1, apart=True)
                src, m = max_out(bk), gr.m
                col, last = 0, None
                for qt, k0, nk in pieces:
                    dg = k0 + nk == qt + 1
                    full = nk - dg
                    if full:
                        last = ve.tensor_reduce(mx[m][:, 1 + (k0 > 0), h, qt:qt + 1], src[:, col:col + full * P],
                                                AX.X, ALU.max)
                    if dg:
                        blk = src[:, col + full * P:col + nk * P]
                        last = ve.tensor_tensor_reduce(blk, blk, cmask[:], 1.0, NEG, ALU.add, ALU.max, mx[m][:, 0, h, qt:qt + 1])
                    col += nk * P
                last.then_inc(S("mr"), 1)

            def max_rows(gr, use):
                g = gr.g
                at(ve, "mr", use)
                ve.tensor_reduce(mall[:], mx[gr.m][:].rearrange("p s h q -> p (h q) s"), AX.X, ALU.max
                                 ).then_inc(S("mall"), 1)
                at(ve, "mall", g + 1)
                ve.tensor_scalar(mneg[:, 0], mall[:], -1.0, None, ALU.mult).then_inc(S("mn0"), 1)
                at(ve, "mn0", g + 1)
                ve.scalar_tensor_tensor(out=mneg[:, 1], in0=mall[:], scalar=-1.0, in1=mneg[:, 0],
                                        op0=ALU.mult, op1=ALU.subtract).then_inc(S("mn"), 1)

            def copy_rows(gr, use, bk):
                at(ve, "mf", use + 1)
                ve.tensor_copy(mrow[gr.m][:], max_out(bk).bitcast(BF16)[0:2 * HG * QT, 0:P]).then_inc(S("mr"), 1)

            def normalise(gr, i, use, bk):
                q0, nq = NORM[i]
                at(ve, "mf", use + 1)
                src = max_out(bk)[:, 0:nq * P].rearrange("p (q h e) -> p q h e", q=nq, h=HG)
                k = len(NORM) * gr.g + i
                ve.reciprocal(rden[:, q0:q0 + nq], src[:, :, :, HD:HD + 1].rearrange("p q h e -> p q (h e)")
                              ).then_inc(S("nm"), 1)
                at(ve, "nm", k + 1)
                at(ve, "yadd", k - len(NORM) + 1)
                ve.tensor_tensor(ynew[:, q0:q0 + nq], src[:, :, :, 0:HD],
                                 rden[:, q0:q0 + nq].unsqueeze(3).to_broadcast([P, nq, HG, HD]), ALU.mult).then_inc(S("mr"), 1)

            def ve_group(gr):
                for it in items(gr)[0]:
                    if it[0] == "max":
                        max_bank(gr.plus(it[1]), it[2], *use_of(gr, it[3]))
                    elif it[0] == "calc":
                        max_rows(gr.plus(1), use_of(gr, it[2])[0])
                    elif it[0] == "rows":
                        copy_rows(gr.plus(1), *use_of(gr, it[2]))
                    elif it[0] == "norm":
                        normalise(gr.plus(-1), it[1], *use_of(gr, it[2]))

            g0, g1, gz = Group(0, 0, 0), Group(1, 1, 0), Group(G - 1, (G - 1) % 3, (G - 1) // 3)
            for w in range(NMX):
                max_bank(g0, w, w, w % MAX_BUFS)
            max_rows(g0, NMX)
            copy_rows(g0, NMX, NMX % MAX_BUFS)
            for w in range(LEAD):
                max_bank(g1, w, NMX + 1 + w, (NMX + 1 + w) % MAX_BUFS)
            drive(ve, ve_group)
            split_low(ve, 0)
            for i in range(len(NORM)):
                normalise(gz, i, USE0[G] + i, (USE0[G] + i) % MAX_BUFS)
            at(ve, "mr", PSM_TOTAL)
            ve.nop().then_inc(S("boundary_c"), 1)
            at(ve, "boundary_c", 4)

            def lo_y(t, m):
                at(ve, "yth", t + 1)
                ve.tensor_tensor(ytl[m][:].rearrange("p c n -> p (c n)"), half(1), yth[m][:].rearrange("p c n -> p (c n)"),
                                 ALU.subtract).then_inc(S("ytl"), 1)

            def lo_x(t, m):
                at(ve, "xth", t + 1)
                ve.tensor_tensor(xtl[m][:].rearrange("p c n -> p (c n)"), half(0), xth[m][:].rearrange("p c n -> p (c n)"),
                                 ALU.subtract).then_inc(S("xtl"), 1)

            def lo_g(t):
                at(ve, "gth", t + 1)
                ve.tensor_tensor(gtl[:].rearrange("p c n -> p (c n)"), bank[3][:], gth[:].rearrange("p c n -> p (c n)"),
                                 ALU.subtract).then_inc(S("gtl"), 1)

            def add_residual(t, m):
                at(ve, "proj", t + 1)
                at(ve, f"xin{m}", 16 * ((t >> 1) + 1) if not isinstance(t, int) else 16 * (t // 2 + 1))
                ve.tensor_tensor(xin[m][:], xin[m][:], half(2), ALU.add).then_inc(S("xs_"), 1)

            def add_ff(t, m):
                at(ve, "ff", t + 1)
                at(ve, "xb", t + 1)
                ve.tensor_tensor(xb[m][:], xb[m][:], half(4 + m), ALU.add).then_inc(S("fs"), 1)

            def norms(j, m):
                sure = not isinstance(j, int)
                work = []
                if sure or j < NTC:
                    add_residual(j, m)
                    at(ve, "xs_", j + 1)
                    work.append((0, xin[m][:], x1[m][:], "x1"))
                if sure or j >= 3:
                    at(ve, "fs", j - 2)
                    work.append((1, xb[1 - m][:], outb[1 - m][:], "fin"))
                k = [NORM_STEPS * j]

                def link(ins, apart=False):
                    ins.then_inc(S("norm"), 1)
                    k[0] = k[0] + 1
                    at(ve, "norm", k[0], apart)

                c0, c1 = work[0][0], work[-1][0] + 1
                v, y, u = (sm[:, o + c0:o + c1] for o in (32, 34, 36))
                for c_, src, _, _ in work:
                    last = ve.bn_stats(sm[:, 16 + 6 * c_:22 + 6 * c_], src)
                link(last, apart=True)
                for c_, _, _, _ in work:
                    last = ve.bn_aggr(sm[:, 28 + 2 * c_:30 + 2 * c_], sm[:, 16 + 6 * c_:22 + 6 * c_])
                link(last)
                var = sm[:, 28:32].rearrange("p (c s) -> p c s", s=2)[:, c0:c1, 1:2].rearrange("p c s -> p (c s)")
                link(ve.tensor_scalar(v, var, EPS, None, ALU.add))
                link(ve.tensor_scalar(y.bitcast(I32), v.bitcast(I32), -0.5, float(0x5F3759DF), ALU.mult, ALU.add))
                for _ in range(NEWTON):
                    link(ve.tensor_tensor(u, y, y, ALU.mult))
                    link(ve.scalar_tensor_tensor(out=u, in0=u, scalar=-0.5, in1=v, op0=ALU.mult, op1=ALU.mult))
                    link(ve.scalar_tensor_tensor(out=y, in0=u, scalar=1.5, in1=y, op0=ALU.add, op1=ALU.mult))
                for c_, src, out, done in work:
                    if done == "x1":
                        at(ve, "xb", j - 1)
                        at(ve, "tx", j - 1)
                    elif sure or j >= 5:
                        at(ve, f"ost{1 - m}", 16 * ((j - 3) >> 1))
                    ve.tensor_scalar(out, src, sm[:, 28 + 2 * c_:29 + 2 * c_], sm[:, 34 + c_:35 + c_],
                                     ALU.subtract, ALU.mult).then_inc(S(done), 1)

            def route(t, m):
                o = 2 * m
                at(ve, "ar", t + 1, apart=True)
                top = sm[:, 48:56]
                ve.max(top, half(3)[:, R:R + E]).then_inc(S("rt"), 1)
                k = 13 * t
                step = [k + 1]

                def link(ins):
                    ins.then_inc(S("rt"), 1)
                    step[0] = step[0] + 1

                def sync():
                    at(ve, "rt", step[0])
                sync()
                ve.tensor_scalar(sm[:, 8 + o:9 + o], top[:, 0:1], -1.0, None, ALU.mult).then_inc(S("nmax"), 1)
                at(ve, "rex", t + 1, apart=True)
                e_ = ex[m][:]
                big = sm[:, 56:64]
                link(ve.max(big, e_))
                sync()
                link(ve.scalar_tensor_tensor(out=rt[:, 0], in0=e_, scalar=big[:, 0:1], in1=rev[:],
                                             op0=ALU.is_equal, op1=ALU.mult))
                sync()
                link(ve.tensor_reduce(sm[:, 64:65], rt[:, 0], AX.X, ALU.max))
                sync()
                link(ve.tensor_scalar(rt[:, 1], rt[:, 0], sm[:, 64:65], None, ALU.is_equal))
                sync()
                link(ve.scalar_tensor_tensor(out=rt[:, 2], in0=rt[:, 1], scalar=-2.0, in1=e_, op0=ALU.mult, op1=ALU.add))
                sync()
                link(ve.scalar_tensor_tensor(out=rt[:, 3], in0=rt[:, 2], scalar=big[:, 1:2], in1=rev[:],
                                             op0=ALU.is_equal, op1=ALU.mult))
                sync()
                link(ve.tensor_reduce(sm[:, 65:66], rt[:, 3], AX.X, ALU.max))
                sync()
                link(ve.scalar_tensor_tensor(out=rt[:, 4], in0=rt[:, 3], scalar=sm[:, 65:66], in1=rt[:, 1],
                                             op0=ALU.is_equal, op1=ALU.add))
                sync()
                link(ve.tensor_tensor(rt[:, 5], rt[:, 4], e_, ALU.mult))
                link(ve.tensor_tensor(sm[:, 66:67], big[:, 0:1], big[:, 1:2], ALU.add))
                sync()
                link(ve.scalar_tensor_tensor(out=sm[:, 67:68], in0=sm[:, 9 + o:10 + o], scalar=1e-6, in1=sm[:, 66:67],
                                             op0=ALU.mult, op1=ALU.add))
                sync()
                link(ve.reciprocal(sm[:, 68:69], sm[:, 67:68]))
                sync()
                at(ve, "g", t - 1)
                ve.tensor_scalar(comb[m][:], rt[:, 5], sm[:, 68:69], 0.5, ALU.mult, ALU.mult).then_inc(S("comb"), 1)
                if isinstance(t, int):
                    assert step[0] == 13 * (t + 1)

            lo_y(0, 0)
            split_low(ve, 1)
            at(ve, "cc_ld", 32)

            def ve_c(j, m):
                sure = not isinstance(j, int)
                if not sure and j == 1:
                    split_low(ve, 2)
                    split_low(ve, 3)
                if sure or j >= 3:
                    add_ff(j - 3, 1 - m)
                if sure or 1 <= j <= NTC:
                    lo_x(j - 1, 1 - m)
                if sure or j >= 2:
                    lo_g(j - 2)
                if sure or 1 <= j <= NTC:
                    route(j - 1, 1 - m)
                norms(j, m)
                if sure or j + 1 < NTC:
                    lo_y(j + 1, 1 - m)

            drive_tiles(ve, ve_c)
            add_ff(NTC - 1, (NTC - 1) % 2)
            norms(NTC + 2, (NTC + 2) % 2)

        @block.tensor
        def _(pe):
            give_head_start(pe, "pe")
            at(pe, "atl", 1)
            for i, (w0, bk) in enumerate(((1, 6), (2, 7))):
                at(pe, "wl", w0 + 1)
                for c_ in range(CC):
                    last = three(pe, half(bk)[0:80], ath[:, c_], atl[:, c_], wh[:, c_, w0 * C:(w0 + 1) * C],
                                 wl[:, c_, w0 * C:(w0 + 1) * C], c_ == 0, c_ == CC - 1)
                last.then_inc(S(("akf", "avf")[i]), 1)
            at(pe, "aks", 1)
            for i in range(4):
                last = pe.transpose(half(6)[:, 80 * i:80 * i + 80], rope[0][0:80, 0, i * P:(i + 1) * P], ident[0:80, 0:80])
            last.then_inc(S("akt"), 1)

            def unit_half(tau, m, j, hf):
                n = 4 * tau + j
                if hf == 0:
                    at(pe, "tm", 4 * (n - 1))
                o = j * 256 + hf * P
                for c_ in range(CC):
                    last = three(pe, half(2 * (j % 2) + hf), wh[:, c_, o:o + P], wl[:, c_, o:o + P],
                                 xh[m][:, c_], xl[m][:, c_], c_ == 0, c_ == CC - 1)
                if hf == 1:
                    last.then_inc(S("uf"), 1)
                return last

            def v_use(tau, w):
                at(pe, "vr", NV * tau + w - 1)
                return half(4 + w % 2)

            def values(tau, m, a_):
                out = v_use(tau, a_)
                for c_ in range(CC):
                    last = three(pe, out, xh[m][:, c_, a_ * P:(a_ + 1) * P], xl[m][:, c_, a_ * P:(a_ + 1) * P],
                                 wh[:, c_, 2 * C:3 * C], wl[:, c_, 2 * C:3 * C], c_ == 0, c_ == CC - 1)
                last.then_inc(S("vf"), 1)

            def a_scores(tau, a_):
                m = 4 * tau + a_
                at(pe, "ro", 4 * tau + 2)
                at(pe, "asub", m - 1)
                for hg in range(2):
                    for hf in range(2):
                        last = pe.matmul(half(6 + a_ % 2)[:, hg * 160:hg * 160 + 160], rope[hg][:, hf, a_ * P:(a_ + 1) * P],
                                         akbd[:, hg, hf].rearrange("p h j -> p (h j)"), start=(hf == 0), stop=(hf == 1))
                last.then_inc(S("as"), 1)

            def a_trans(tau, a_, w):
                out = v_use(tau, w)
                at(pe, "ad", 5 * (4 * tau + a_ + 1))
                src = pa[a_][:].rearrange("p h j -> p (h j)")
                for i in range(4):
                    last = pe.transpose(out[0:80, i * P:(i + 1) * P], src[:, 80 * i:80 * i + 80], ident[:])
                last.then_inc(S("vf"), 1)

            def a_out(tau, a_, w):
                out = v_use(tau, w)
                at(pe, "vr", NV * tau + w - 1)
                for i in range(4):
                    last = pe.matmul(out[:, i * P:(i + 1) * P], pat[a_ % 2][:, i], avbd[:, i], start=True, stop=True)
                last.then_inc(S("vf"), 1)

            at(pe, "wl", 3)
            at(pe, "akbd", 4)
            with pe.Fori(0, NB) as b:
                for u in range(NTT):
                    tau = NTT * b + u
                    at(pe, "xl", 2 * (tau + 1))
                    for j in range(2):
                        unit_half(tau, u, j, 0)
                        unit_half(tau, u, j, 1)
                    for a_ in range(4):
                        values(tau, u, a_)
                    for a_ in range(3):
                        a_scores(tau, a_)
                    unit_half(tau, u, 2, 0)
                    a_scores(tau, 3)
                    unit_half(tau, u, 2, 1)
                    a_trans(tau, 0, 4)
                    a_trans(tau, 1, 5)
                    unit_half(tau, u, 3, 0)
                    a_out(tau, 0, 6)
                    a_out(tau, 1, 7)
                    a_trans(tau, 2, 8)
                    a_trans(tau, 3, 9)
                    unit_half(tau, u, 3, 1)
                    a_out(tau, 2, 10)
                    a_out(tau, 3, 11)
            at(pe, "vf", NV * TILES)
            pe.nop().then_inc(S("boundary_b"), 1)
            at(pe, "tm", 4 * NU * TILES)
            at(pe, "vr", NV * TILES)

            def free_bank(use, apart=False):
                at(pe, "mr", use + 1 - MAX_BUFS, apart)

            def score(gr, st, h, c):
                m, kb = gr.m, ORDER[st]
                if st == 0 and h == 0 and c == 0:
                    at(pe, f"mrow{m}", 16 * (gr.v + 1))
                n, bk, c0, w = list(score_chunks(gr, st, h))[c]
                if not (gr.fixed and n < SCORE_BUFS):
                    at(pe, "ex", n + 1 - SCORE_BUFS)
                pe.matmul(half(bk)[:, 0:w], ks[m][0:KX, h, kb * P:(kb + 1) * P],
                          qs[m][0:KX, h, kb * P + c0:kb * P + c0 + w], start=True, stop=True).then_inc(S("sc"), 1)

            def max_scores(gr, w, use, bk):
                h, m = w // NMB, gr.m
                if w == 0:
                    at(pe, f"grp{m}", 16 * GROUP_LOADS * (gr.v + 1))
                free_bank(use)
                out, col = max_out(bk), 0
                for qt, k0, nk in MAX_BANKS[w % NMB]:
                    last = pe.matmul(out[:, col:col + nk * P], qs[m][0:KR, h, qt * P:(qt + 1) * P],
                                     ks[m][0:KR, h, k0 * P:(k0 + nk) * P], start=True, stop=True)
                    col += nk * P
                last.then_inc(S("mf"), 1)

            def trans_rows(gr, use, bk):
                at(pe, "mn", gr.g + 1)
                free_bank(use, apart=True)
                pe.transpose(max_out(bk).bitcast(BF16)[0:2 * HG * QT, 0:P], mneg[:].rearrange("p s n -> p (s n)"),
                             identb[:]).then_inc(S("mf"), 1)

            def trans_out(gr, i, use, bk):
                q0, nq = NORM[i]
                at(pe, "yts", 2 * gr.g + 1 + (q0 + nq - 1) * P // BANK)
                free_bank(use)
                for q in range(nq):
                    last = pe.transpose(max_out(bk)[:, q * P:(q + 1) * P], yts[:, (q0 + q) * P:(q0 + q + 1) * P],
                                        ident[:])
                last.then_inc(S("mf"), 1)

            def weighted(gr, kb, q0, q1):
                st = ORDER.index(kb)
                if st == 0 and q0 == 0:
                    at(pe, "vb", gr.g + 1)
                if st == 0:
                    at(pe, "yts", 2 * gr.g - 1 + q0 // BANK)
                if q0 == kb * P:
                    at(pe, "dg", QT * gr.g + st + 1)
                src = pt[(QT * gr.m + st) % 3]
                for h in range(HG):
                    last = pe.matmul(bank[3][VW * h:VW * h + VW, q0:q1], vb[gr.m][:, kb, h, :],
                                     src[:, h, q0:q1], start=(st == 0), stop=(kb == LAST_TILE[q0 // BANK]))
                if q1 == T:
                    last.then_inc(S("pv"), 1)

            def pe_group(gr):
                for it in items(gr)[0]:
                    if it[0] == "score":
                        score(gr, *it[1:])
                    elif it[0] == "max":
                        max_scores(gr.plus(it[1]), it[2], *use_of(gr, it[3]))
                    elif it[0] == "rows":
                        trans_rows(gr.plus(1), *use_of(gr, it[2]))
                    elif it[0] == "norm":
                        trans_out(gr.plus(-1), it[1], *use_of(gr, it[2]))
                    elif it[0] == "pv":
                        weighted(gr.plus(it[1]), *it[2:])

            g0, g1, gz = Group(0, 0, 0), Group(1, 1, 0), Group(G - 1, (G - 1) % 3, (G - 1) // 3)
            for w in range(NMX):
                max_scores(g0, w, w, w % MAX_BUFS)
            trans_rows(g0, NMX, NMX % MAX_BUFS)
            for w in range(LEAD):
                max_scores(g1, w, NMX + 1 + w, (NMX + 1 + w) % MAX_BUFS)
            at(pe, "vset", 9)
            drive(pe, pe_group)
            for kb in ORDER[QT - LAG:]:
                for piece in value_pieces(kb):
                    weighted(gz, kb, *piece)
            for i in range(len(NORM)):
                trans_out(gz, i, USE0[G] + i, (USE0[G] + i) % MAX_BUFS)
            at(pe, "mf", PSM_TOTAL)
            pe.nop().then_inc(S("boundary_c"), 1)
            at(pe, "boundary_c", 4)

            def t_y(t, m):
                at(pe, "yt", t + 1)
                at(pe, "ytl", t)
                for c_ in range(CC):
                    last = pe.transpose(half(1)[:, c_ * P:(c_ + 1) * P], ytile[m][:, c_ * P:(c_ + 1) * P], ident[:])
                last.then_inc(S("ty"), 1)

            def proj(t, m):
                at(pe, "ytl", t + 1)
                at(pe, "xs_", t)
                at(pe, "cwl", 1)
                for c_ in range(CC):
                    last = three(pe, half(2), yth[m][:, c_], ytl[m][:, c_], wph[:, c_], wpl[:, c_], c_ == 0, c_ == CC - 1)
                last.then_inc(S("proj"), 1)

            def t_x(t, m):
                at(pe, "x1", t + 1)
                at(pe, "xtl", t)
                for c_ in range(CC):
                    last = pe.transpose(half(0)[:, c_ * P:(c_ + 1) * P], x1[m][:, c_ * P:(c_ + 1) * P], ident[:])
                last.then_inc(S("tx"), 1)

            def t_g(t, m):
                at(pe, "g", t + 1)
                at(pe, "gtl", t)
                gf = gbuf[m][:].rearrange("p e r -> p (e r)")
                for c_ in range(8):
                    last = pe.transpose(bank[3][:, c_ * P:(c_ + 1) * P], gf[:, c_ * P:(c_ + 1) * P], ident[:])
                last.then_inc(S("tg"), 1)

            def ar(t, m):
                at(pe, "xtl", t + 1)
                at(pe, "rex", t)
                at(pe, "hr", t)
                at(pe, "ar_ld", 16)
                for c_ in range(CC):
                    for part_ in (xth[m], xtl[m]):
                        last = pe.matmul(half(3)[:, 0:R + E], part_[:, c_].bitcast(F32), ar_w[:, c_],
                                         start=(c_ == 0 and part_ is xth[m]), stop=(c_ == CC - 1 and part_ is xtl[m]))
                last.then_inc(S("ar"), 1)

            def base(t, m):
                at(pe, "fs", t - 1)
                at(pe, "cwl", 2)
                for c_ in range(CC):
                    three(pe, half(4 + m), xth[m][:, c_], xtl[m][:, c_], wfh[:, c_], wfl[:, c_], c_ == 0, False)

            def delta(t, m):
                at(pe, "gtl", t + 1)
                at(pe, "cwl", 4)
                for c_ in range(8):
                    last = three(pe, half(4 + m), gth[:, c_], gtl[:, c_], wbh[:, c_], wbl[:, c_], False, c_ == 7)
                last.then_inc(S("ff"), 1)

            t_y(0, 0)

            def pe_c(j, m):
                sure = not isinstance(j, int)
                if sure or 1 <= j <= NTC:
                    t_x(j - 1, 1 - m)
                if sure or j >= 2:
                    t_g(j - 2, m)
                if sure or j + 1 < NTC:
                    t_y(j + 1, 1 - m)
                if sure or 1 <= j <= NTC:
                    ar(j - 1, 1 - m)
                if sure or j < NTC:
                    proj(j, m)
                if sure or 1 <= j <= NTC:
                    base(j - 1, 1 - m)
                if sure or j >= 2:
                    delta(j - 2, m)

            drive_tiles(pe, pe_c)


def constants():
    import numpy as np

    theta = np.float32(1.0) / np.power(np.float32(10000.0), (np.arange(0, HD, 2, dtype=np.float32) / np.float32(HD)))
    angle = np.outer(np.arange(T, dtype=np.float32), theta.astype(np.float32)).astype(np.float32)
    cs = np.stack([np.cos(angle.astype(np.float64)), np.sin(angle.astype(np.float64))]).astype(np.float32)
    p = np.arange(P)
    a = np.arange(8 * J)
    return {
        "cos_sin": np.ascontiguousarray(cs[:, :, p % 8].transpose(2, 0, 1)),
        "ident": np.eye(P, dtype=np.float32),
        "akm": (p[:, None] // 8 == np.arange(16)).astype(np.float32),
        "avm": (a[:, None] // J == np.arange(8)).astype(np.float32),
        "cmask": np.where(p[None, :] <= p[:, None], 0.0, NEG).astype(np.float32),
        "rev": np.ascontiguousarray(np.broadcast_to(np.arange(E, 0, -1, dtype=np.float32), (P, E))),
    }


def kernel(L0_attn_x, L0_attn_w_attn, L0_attn_w_proj, L0_attn_adapter_wte, L0_attn_gating, L0_ffn_base_w,
           L0_ffn_base_b, L0_ffn_A, L0_ffn_B, L0_ffn_router_w):
    import numpy as np
    import concourse.bacc as bacc
    from concourse.bass_utils import run_bass_kernel_spmd

    x = np.asarray(L0_attn_x).reshape(NB * T, C)
    w = np.asarray(L0_attn_w_attn)
    qk = w[:2 * C].reshape(2, 2, 16, 2, 8, C).transpose(0, 1, 3, 2, 4, 5).reshape(2 * C, C)
    arrays = {
        "x": x,
        "xT": x.T,
        "w_attnT": np.concatenate([qk, w[2 * C:]]).T,
        "w_projT": np.asarray(L0_attn_w_proj).T,
        "adapterT": np.asarray(L0_attn_adapter_wte).T,
        "gating": np.asarray(L0_attn_gating),
        "base_wT": np.asarray(L0_ffn_base_w).T,
        "base_b": np.asarray(L0_ffn_base_b),
        "arT": np.concatenate([np.asarray(L0_ffn_A), np.asarray(L0_ffn_router_w)]).T,
        "B_T": np.asarray(L0_ffn_B).transpose(0, 2, 1).reshape(E * R, C),
    }
    arrays.update(constants())
    arrays = {k: np.ascontiguousarray(v) for k, v in arrays.items()}
    nc = bacc.Bacc("TRN2", target_bir_lowering=False, num_devices=1)
    d = {k: nc.dram_tensor("in_" + k, v.shape, mybir.dt.from_np(v.dtype), kind="ExternalInput").ap() for k, v in arrays.items()}
    d["out"] = nc.dram_tensor("out", (NB * T, C), F32, kind="ExternalOutput").ap()
    build(nc, d)
    r = run_bass_kernel_spmd(nc, [{"in_" + k: v for k, v in arrays.items()}], core_ids=[0])
    return r.results[0]["out"].reshape(NB, T, C)
```
